# Optimizing a Trainium2 kernel written in Bass

```python
import numpy as np
import jax
import jax.numpy as jnp

def _softmax(x, axis=-1):
    return jax.nn.softmax(x, axis=axis)

def _gelu(x):
    return jax.nn.gelu(x, approximate=True)

def _silu(x):
    return jax.nn.silu(x)

def _sigmoid(x):
    return jax.nn.sigmoid(x)

def _layernorm(x, axis=-1, eps=1e-05):
    m = jnp.mean(x, axis=axis, keepdims=True)
    v = jnp.var(x, axis=axis, keepdims=True)
    return (x - m) / jnp.sqrt(v + eps)

def _scatter_add(tgt, idx, src, axis=0):
    return tgt.at[idx].add(src)

def _segment_sum(src, seg, n):
    return jax.ops.segment_sum(src, seg, n)
kernel_name = 'mk_flamingo_gated_d1_seqx_r8_be3f0d'

def setup_inputs(seed: int=0):
    np.random.seed(seed)
    _w = jnp.asarray

    def _rec_inputs():
        import jax
        import jax.numpy as jnp
        _rk = jax.random.key(seed)
        x = -0.0002928 + 1 * jax.random.normal(jax.random.fold_in(_rk, 1), (128, 64, 128), jnp.float32)
        _lenS = 64 - jax.random.randint(jax.random.fold_in(_rk, 7), (128,), 0, max(1, 64 // 4) + 1, jnp.int32)
        _lenS2 = 64 - jax.random.randint(jax.random.fold_in(_rk, 8), (128,), 0, max(1, 64 // 4) + 1, jnp.int32)
        _ctx_1024P = jax.random.normal(jax.random.fold_in(_rk, 11), (128, 16, 128), jnp.float32)
        _ctx_1024c = jax.random.dirichlet(jax.random.fold_in(_rk, 511), 0.3 * jnp.ones((16,), jnp.float32), (128, 64))
        _ctx_1024t = jnp.einsum('bsk,bkd->bsd', _ctx_1024c, _ctx_1024P)
        _ctx_1024t = _ctx_1024t * jax.lax.rsqrt(jnp.mean(jnp.square(_ctx_1024t)) + 1e-12) * 0.953939
        ctx_1024 = 4.13588e-05 + 0.999923 * (_ctx_1024t + 0.3 * jax.random.normal(jax.random.fold_in(_rk, 611), (128, 64, 128), jnp.float32))
        itok_BxS_8_8191 = jax.random.randint(jax.random.fold_in(_rk, 12), (128, 64), 8, 1024, jnp.int32)
        itok_BxS2_1_8191 = jax.random.randint(jax.random.fold_in(_rk, 13), (128, 64), 1, 1024, jnp.int32)
        _validS = jnp.arange(64)[None, :] < _lenS[:, None]
        _validS2 = jnp.arange(64)[None, :] < _lenS2[:, None]
        _causal = jnp.tril(jnp.ones((64, 64), dtype=bool))
        mask_BxSxS2_if1 = jnp.where(jnp.ones((128, 64, 64), dtype=bool), 1, 0).astype(jnp.int32)
        _g = jax.random.normal(jax.random.fold_in(_rk, 9001), (2, 1), jnp.float32)
        _g = jnp.sign(_g) * jnp.maximum(jnp.abs(_g), 1.0) + (_g == 0) * 1.0
        g_xattn = _g[0]
        g_ffn = _g[1]
        return (x, ctx_1024, itok_BxS_8_8191, itok_BxS2_1_8191, mask_BxSxS2_if1, g_xattn, g_ffn)
    x, ctx_1024, itok_BxS_8_8191, itok_BxS2_1_8191, mask_BxSxS2_if1, g_xattn, g_ffn = _rec_inputs()

    def _L0_xattn_setup():
        import jax, jax.numpy as jnp
        import numpy as np
        DIM = 128
        NUM_HEADS = 16
        HEAD_DIM = DIM // NUM_HEADS

        def _slopes(num_heads):
            ratio = 2.0 ** (-8.0 / num_heads)
            return jnp.asarray([ratio ** i for i in range(1, num_heads + 1)], dtype=jnp.float32)
        key = jax.random.key(seed)
        ks = jax.random.split(key, 10)
        b, q_len, k_len = (2, 256, 512)
        query = jax.random.normal(ks[0], (b, q_len, DIM), dtype=jnp.float32)
        keys = jax.random.normal(ks[1], (b, k_len, DIM), dtype=jnp.float32)
        values = jax.random.normal(ks[2], (b, k_len, DIM), dtype=jnp.float32)
        query_pos = jnp.sort(jax.random.randint(ks[3], (b, q_len), 0, 1024), axis=-1)
        key_pos = jnp.sort(jax.random.randint(ks[4], (b, k_len), 0, 1024), axis=-1)
        mask = jnp.ones((b, q_len, k_len), dtype=jnp.int32)
        lim = float(np.sqrt(6.0 / (DIM + DIM)))
        W_q = jax.random.uniform(ks[5], (DIM, DIM), minval=-lim, maxval=lim, dtype=jnp.float32)
        W_k = jax.random.uniform(ks[6], (DIM, DIM), minval=-lim, maxval=lim, dtype=jnp.float32)
        W_v = jax.random.uniform(ks[7], (DIM, DIM), minval=-lim, maxval=lim, dtype=jnp.float32)
        W_o = jax.random.uniform(ks[8], (DIM, DIM), minval=-lim, maxval=lim, dtype=jnp.float32)
        return {'query': query, 'keys': keys, 'values': values, 'W_q': W_q, 'W_k': W_k, 'W_v': W_v, 'W_o': W_o, 'query_pos': query_pos, 'key_pos': key_pos, 'mask': mask}
    _L0_xattn_all = _L0_xattn_setup()
    _L0_xattn_in = {k: v for k, v in _L0_xattn_all.items() if k in ('W_q', 'W_k', 'W_v', 'W_o')}
    del _L0_xattn_all

    def _L0_ffn_setup():
        import jax, jax.numpy as jnp
        import numpy as np
        TOPK = 8
        BN_EPS = 1e-05
        key = jax.random.key(seed)
        ks = jax.random.split(key, 5)
        b, n, d = (2, 128, 128)
        h, nk, kd = (8, 32, 128)
        ne = nk * nk
        scale = 0.02
        return {'inputs': jax.random.normal(ks[0], (b, n, d), jnp.float32), 'gamma': jnp.ones((d,), jnp.float32), 'beta': jnp.zeros((d,), jnp.float32), 'w_q': jax.random.normal(ks[1], (2 * h * kd, d), jnp.float32) * scale, 'keys': jax.random.normal(ks[2], (h, nk, 2, kd), jnp.float32) * scale, 'key_in': jax.random.normal(ks[3], (ne, d), jnp.float32) * scale, 'key_out': jax.random.normal(ks[4], (ne, d), jnp.float32) * scale}
    _L0_ffn_all = _L0_ffn_setup()
    _L0_ffn_in = {k: v for k, v in _L0_ffn_all.items() if k in ('gamma', 'beta', 'w_q', 'keys', 'key_in', 'key_out')}
    del _L0_ffn_all
    return {'x': x, 'ctx_1024': ctx_1024, 'itok_BxS_8_8191': itok_BxS_8_8191, 'itok_BxS2_1_8191': itok_BxS2_1_8191, 'mask_BxSxS2_if1': mask_BxSxS2_if1, 'g_xattn': g_xattn, 'g_ffn': g_ffn, 'L0_xattn_W_q': _L0_xattn_in['W_q'], 'L0_xattn_W_k': _L0_xattn_in['W_k'], 'L0_xattn_W_v': _L0_xattn_in['W_v'], 'L0_xattn_W_o': _L0_xattn_in['W_o'], 'L0_ffn_gamma': _L0_ffn_in['gamma'], 'L0_ffn_beta': _L0_ffn_in['beta'], 'L0_ffn_w_q': _L0_ffn_in['w_q'], 'L0_ffn_keys': _L0_ffn_in['keys'], 'L0_ffn_key_in': _L0_ffn_in['key_in'], 'L0_ffn_key_out': _L0_ffn_in['key_out']}

def reference(x, ctx_1024, itok_BxS_8_8191, itok_BxS2_1_8191, mask_BxSxS2_if1, g_xattn, g_ffn, L0_xattn_W_q, L0_xattn_W_k, L0_xattn_W_v, L0_xattn_W_o, L0_ffn_gamma, L0_ffn_beta, L0_ffn_w_q, L0_ffn_keys, L0_ffn_key_in, L0_ffn_key_out):
    import jax
    import jax.numpy as jnp

    def _L0_xattn_ref(query, keys, values, W_q, W_k, W_v, W_o, query_pos, key_pos, mask):
        import jax, jax.numpy as jnp
        import numpy as np
        DIM = 128
        NUM_HEADS = 16
        HEAD_DIM = DIM // NUM_HEADS

        def _slopes(num_heads):
            ratio = 2.0 ** (-8.0 / num_heads)
            return jnp.asarray([ratio ** i for i in range(1, num_heads + 1)], dtype=jnp.float32)
        b, q_len, _ = query.shape
        k_len = keys.shape[1]
        scale = 1.0 / np.sqrt(HEAD_DIM)
        Q = (query @ W_q.T).reshape(b, q_len, NUM_HEADS, HEAD_DIM).transpose(0, 2, 1, 3)
        K = (keys @ W_k.T).reshape(b, k_len, NUM_HEADS, HEAD_DIM).transpose(0, 2, 1, 3)
        V = (values @ W_v.T).reshape(b, k_len, NUM_HEADS, HEAD_DIM).transpose(0, 2, 1, 3)
        scores = jnp.einsum('bhqd,bhkd->bhqk', Q, K) * scale
        dist = (query_pos[:, :, None] - key_pos[:, None, :]).astype(scores.dtype)
        bias = -_slopes(NUM_HEADS)[None, :, None, None] * dist[:, None, :, :]
        scores = scores + bias
        scores = jnp.where(mask[:, None, :, :] == 0, -jnp.inf, scores)
        m = jnp.max(scores, axis=-1, keepdims=True)
        e = jnp.exp(scores - m)
        attn = e / (1.0 + jnp.sum(e, axis=-1, keepdims=True))
        out = jnp.einsum('bhqk,bhkd->bhqd', attn, V)
        out = out.transpose(0, 2, 1, 3).reshape(b, q_len, DIM)
        return out @ W_o.T

    def _L0_ffn_ref(inputs, gamma, beta, w_q, keys, key_in, key_out):
        import jax, jax.numpy as jnp
        import numpy as np
        TOPK = 8
        BN_EPS = 1e-05
        b, n, d = inputs.shape
        h, nk, _, kd = keys.shape
        k = TOPK
        x = inputs.reshape(b * n, d)
        mu = jnp.mean(x, axis=0)
        var = jnp.mean(jnp.square(x - mu), axis=0)
        xn = (x - mu) * jax.lax.rsqrt(var + BN_EPS) * gamma + beta
        q = (xn @ w_q.T).reshape(b, n, 2, h, kd).transpose(2, 0, 1, 3, 4)
        sim = jnp.einsum('pbnhd,hkpd->pbnhk', q, keys)
        s, i = jax.lax.top_k(sim, k)
        sx, sy = (s[0], s[1])
        ix, iy = (i[0], i[1])
        all_scores = (sx[..., :, None] + sy[..., None, :]).reshape(b, n, h, k * k)
        all_idx = (ix[..., :, None] * nk + iy[..., None, :]).reshape(b, n, h, k * k)
        scores, pk = jax.lax.top_k(all_scores, k)
        idx = jnp.take_along_axis(all_idx, pk, axis=-1)
        w_down = key_in[idx]
        w_up = key_out[idx]
        o = jnp.einsum('bnd,bnhkd->bnhk', inputs, w_down)
        o = jax.nn.gelu(o, approximate=False) * jax.nn.softmax(scores, axis=-1)
        return jnp.einsum('bnhk,bnhkd->bnd', o, w_up)
    x = x + jnp.tanh(g_xattn[0]) * _L0_xattn_ref(_layernorm(x, axis=-1), ctx_1024, ctx_1024, L0_xattn_W_q, L0_xattn_W_k, L0_xattn_W_v, L0_xattn_W_o, itok_BxS_8_8191, itok_BxS2_1_8191, mask_BxSxS2_if1)
    x = x + jnp.tanh(g_ffn[0]) * _L0_ffn_ref(_layernorm(x, axis=-1), L0_ffn_gamma, L0_ffn_beta, L0_ffn_w_q, L0_ffn_keys, L0_ffn_key_in, L0_ffn_key_out)
    return x

_drawn_inputs = setup_inputs


def setup_inputs(seed=0):
    import zlib

    import numpy as np

    out = dict(_drawn_inputs(seed))
    spreads = {'L0_ffn_gamma': (1.0, 0.6), 'L0_ffn_beta': (0.0, 0.8)}
    factors = {'L0_ffn_w_q': 8.0, 'L0_ffn_keys': 8.0, 'L0_ffn_key_in': 8.0, 'L0_ffn_key_out': 8.0}
    for name, (base, spread) in spreads.items():
        noise = np.random.default_rng([zlib.crc32(name.encode()), seed]).standard_normal(out[name].shape)
        drawn = base * np.exp(spread * noise) if base else spread * noise
        out[name] = jnp.asarray(drawn.astype(out[name].dtype))
    for name, factor in factors.items():
        out[name] = (out[name] * factor).astype(out[name].dtype)
    return out
```

```python
import concourse.bass as bass
from concourse import mybir
from contextlib import ExitStack
import numpy as np

F32 = mybir.dt.float32
BF16 = mybir.dt.bfloat16
F16 = mybir.dt.float16
I32 = mybir.dt.int32
U16 = mybir.dt.uint16
ALU = mybir.AluOpType
ACT = mybir.ActivationFunctionType
AX = mybir.AxisListType

P = 128
B, S, D = 128, 64, 128
T = B * S // P
H, HD = 16, 8
HG = H // 4
HP = H // 2
FH, NK, K8 = 8, 32, 8
LO = NK * NK // P
QROWS, KROWS = 9, 6
ROWS = QROWS + KROWS
G4 = 4
HALF = P // 2
MASKED = -1.0e30
EPS = 1e-5
W_SCALE = 2.0 ** 14
W2_SCALE = 2.0 ** 11
SLOPES = [float(np.float32((2.0 ** (-8.0 / H)) ** i)) for i in range(1, H + 1)]


def bf16_parts(v):
    out, rest = [], np.asarray(v, np.float32)
    for _ in range(3):
        top = (rest.view(np.uint32) & np.uint32(0xFFFF0000)).view(np.float32)
        out.append(top)
        rest = rest - top
    return out


def shape_constants():
    s = bf16_parts(-np.asarray(SLOPES, np.float32))
    slope_rows = np.stack([np.repeat(s[j], S) for _ in range(3) for j in range(3)])
    of_batch = np.zeros((KROWS, P), np.float32)
    of_batch[0:3, 0:S] = 1.0
    of_batch[3:6, S:P] = 1.0
    return np.ascontiguousarray(slope_rows, np.float32), of_batch


def wait(eng, sem, value):
    if not (isinstance(value, int) and value <= 0):
        eng.wait_ge(sem, value)


def steps(eng, body, n, lead=2, tail=2):
    for i in range(lead):
        body(i, i // 2, i % 2)
    with eng.Fori(lead // 2, (n - tail) // 2) as j:
        for par in range(2):
            body(2 * j + par, j, par)
    for i in range(n - tail, n):
        body(i, i // 2, i % 2)


class Chain:

    def __init__(self, eng, sem, start=0):
        self.eng, self.sem, self.base, self.n = eng, sem, start, 0

    def at(self, base):
        self.base, self.n = base, 0

    def add(self, ins):
        self.n += 1
        ins.then_inc(self.sem, 1)

    def settle(self):
        self.eng.wait_ge(self.sem, self.base + self.n)

    def link(self, ins):
        self.add(ins)
        self.settle()


def rows(ap, count):
    s = list(ap.shape)
    return ap.unsqueeze(len(s)).broadcast_to(s + [count])


def gated_block(nc, x, ctx, qpos, kpos, mask, g_x, g_f, wq, wk, wv, wo, gamma, beta, w_ffn, keys,
                key_in, key_out, slope_rows, of_batch, out):
    x_t = x.rearrange("(i c) s d -> (c s) i d", c=2)
    ctx_t = ctx.rearrange("(i c) s d -> i (c s) d", c=2)
    mask_t = mask.rearrange("(i c) q k -> (c q) i k", c=2)
    out_t = out.rearrange("(i c) s d -> (c s) i d", c=2)
    krows_d = nc.dram_tensor("krows_d", (B, 3, H * S), BF16, kind="Internal").ap()
    qrows_d = nc.dram_tensor("qrows_d", (B, 3, 3, S), BF16, kind="Internal").ap()
    krows_t = krows_d.rearrange("(i c) p n -> i (c p) n", c=2)
    qrows_t = qrows_d.rearrange("(i c) a b q -> i (a b) c q", c=2)

    es = ExitStack()
    with es:
        def sb(name, shape, dt=F32):
            return es.enter_context(nc.sbuf_tensor(name, shape, dt))[:]

        def sem(name):
            return es.enter_context(nc.semaphore(name))

        X = sb("X", [P, T, D])
        ZT = sb("ZT", [P, T * P])
        idf = sb("idf", [P, P])
        idb = sb("idb", [P, P], BF16)
        stats = sb("stats", [P, T, 6])
        lnt = sb("lnt", [P, 3, T])
        mean = sb("mean", [P, T])
        rstd = sb("rstd", [P, T])
        W2 = sb("W2", [P, 2 * FH * NK])
        kinT = sb("kinT", [P, LO, P])
        kout = sb("kout", [P, LO, D])
        gates = sb("gates", [P, 4])
        bn = sb("bn", [P, 8])
        A = sb("A", [P, 2, P, HALF], F16)
        WORDS = 22528
        AR = sb("AR", [P, WORDS])

        def carver(area, total, start=0):
            at = [start]

            def carve(shape, dt=F32):
                n = int(np.prod(shape[1:]))
                words = n if dt in (F32, I32) else (n + 1) // 2
                v = area[0:shape[0], at[0]:at[0] + words]
                at[0] += (words + 7) // 8 * 8
                assert at[0] <= total, at[0]
                if dt != F32:
                    v = v.bitcast(dt)
                if len(shape) > 2:
                    names = "abcd"[:len(shape) - 1]
                    v = v.rearrange(f"p ({' '.join(names)}) -> p {' '.join(names)}",
                                    **{c: shape[1 + q] for q, c in enumerate(names)})
                return v
            return carve, at

        carve, _ = carver(AR, WORDS)
        WqT = carve([P, HG, 4, 32])
        WkT = carve([P, HG, 4, 32])
        WvT = carve([P, D])
        WoT = carve([P, D])
        maskI = carve([P, T, S], I32)
        cb = [carve([P, D]) for _ in range(2)]
        xnb = [carve([P, D]) for _ in range(2)]
        lrow = [carve([ROWS, P], BF16) for _ in range(2)]
        rrow = [carve([ROWS, H * S], BF16) for _ in range(2)]
        mb = [carve([P, S], BF16) for _ in range(2)]
        xcT = carve([P, 2, P])
        Qp = carve([P, HG, P])
        Kp = carve([P, HG, P])
        Vb = [carve([P, 2, HP, 2, HD + 1]) for _ in range(2)]
        E = carve([P, H, S])
        ET = carve([P, HP, P])
        smax = carve([P, H])
        den = carve([P, H])
        attn = carve([P, H, HD])
        aT = carve([P, P])
        zcarve, _ = carver(ZT, T * P)
        wnat = zcarve([P, 4, D])
        wfn = A.rearrange("p a v t -> p (a v t)").bitcast(F32)[:, 0:2 * FH * D].rearrange("p (m d) -> p m d", d=D)
        keyn = zcarve([P, 2, 2, D])
        keyT = zcarve([P, 2, 2, P])
        kinn = zcarve([P, LO, D])
        posI = zcarve([P, 2, S], I32)
        posF = zcarve([P, 2, S])
        kbias = zcarve([P, H, S])
        kparts = zcarve([P, 3, H * S], BF16)
        qparts = zcarve([P, 3, S], BF16)
        srow_f = zcarve([QROWS, H * S])
        brow_f = zcarve([KROWS, P])
        brow_b = zcarve([KROWS, P], BF16)
        carve, at = carver(AR, WORDS)
        iota = carve([P, P, HALF], F16)
        iotaL = carve([P, LO, P], F16)
        hi16 = carve([P, T // 2, P], F16)
        lo16 = carve([P, T // 2, P], F16)
        w1 = carve([P, T // 2, P], F16)
        w2 = carve([P, T // 2, P], F16)
        shared = at[0]
        zb = [carve([P, 4, D]) for _ in range(2)]
        xs = [carve([P, P]) for _ in range(2)]
        sim = [carve([P, 2, FH, NK]) for _ in range(2)]
        s8 = [carve([P, 2, FH, K8]) for _ in range(2)]
        i8 = carve([P, 2, G4 * FH, K8], U16)
        i8f = carve([P, 2, G4 * FH, K8], F16)
        cand = [carve([P, FH, K8, K8]) for _ in range(2)]
        val = carve([P, G4 * FH, K8])
        pk = carve([P, G4 * FH, K8], U16)
        pab = carve([P, 2, G4 * FH, K8], U16)
        planes = carve([P, 2 * K8, G4 * FH, K8], F16)
        tree = carve([P, K8, G4 * FH, K8], F16)
        code = carve([P, G4 * FH, K8])
        wgt = carve([P, G4 * FH, K8])
        wnorm = carve([P, G4 * FH, K8])
        wsum = carve([P, G4 * FH])
        codeT = carve([P, 2, P], U16)
        codeHL = carve([P, 2, 2, P], U16)
        wT = carve([P, 2, P])
        wRest = carve([P, 2, P])
        carve, at = carver(AR, WORDS, shared)
        Bm = [carve([P, 2, LO, P], F16) for _ in range(2)]
        oh = carve([P, LO, P], F16)
        GG = [carve([P, LO, 2, P]) for _ in range(2)]
        p2 = [carve([P, LO, HALF]) for _ in range(2)]
        Pt = [carve([P, LO, HALF]) for _ in range(2)]
        yb = [carve([P, 2, D]) for _ in range(2)]

        PS = es.enter_context(nc.psum_tensor("PS", [P, 8, 512], F32))[:]

        in_x, in_w, in_p, in_m = (sem("in_" + n) for n in "xwpm")
        ids, zeros, const_rows, prep = sem("ids"), sem("zeros"), sem("const_rows"), sem("prep")
        w_T, w_T_sb, w2_ps, w2_sb, gates_ok = (sem(n) for n in ("w_T", "w_T_sb", "w2_ps", "w2_sb", "gates_ok"))
        parts_ok, parts_out, std_in, std_out = (sem(n) for n in ("parts_ok", "parts_out", "std_in", "std_out"))
        ctx_in = [sem(f"ctx_in{n}") for n in range(2)]
        rows_in = [sem(f"rows_in{n}") for n in range(2)]
        xn_ready, in_T, in_T_sb = sem("xn_ready"), sem("in_T"), sem("in_T_sb")
        q_ps, k_ps, v_ps, q_sb, k_sb, v_sb = (sem(n) for n in ("q_ps", "k_ps", "v_ps", "q_sb", "k_sb", "v_sb"))
        mask_ok, shifted, probs = (sem(n) for n in ("mask_ok", "shifted", "probs"))
        e_T, e_T_sb, av_ok, attn_ok = (sem(n) for n in ("e_T", "e_T_sb", "av_ok", "attn_ok"))
        attn_T, attn_T_sb, wo_ok, x2_ok, stat_ok = (
            sem(n) for n in ("attn_T", "attn_T_sb", "wo_ok", "x2_ok", "stat_ok"))
        dve0, dve1, dve2, dve3 = (sem(f"dve{n}") for n in range(4))
        z_ok, z_T, z_sb, z_stat, bn_ok = (sem(n) for n in ("z_ok", "z_T", "z_sb", "z_stat", "bn_ok"))
        xs_ok, sim_ps, sim_sb, sim_used = (sem(n) for n in ("xs_ok", "sim_ps", "sim_sb", "sim_used"))
        diff_ok, exp_ok, picks_ok, picks_T, picks_sb, lists_ok = (
            sem(n) for n in ("diff_ok", "exp_ok", "picks_ok", "picks_T", "picks_sb", "lists_ok"))
        iota_ok = sem("iota_ok")
        a_ok, p_ps, p2_sb, pt_ok, g_ok = (sem(n) for n in ("a_ok", "p_ps", "p2_sb", "pt_ok", "g_ok"))
        o_ps, gel_sb, f_ps, y_ok = (sem(n) for n in ("o_ps", "gel_sb", "f_ps", "y_ok"))
        row_tile = sem("row_tile")
        oh_ok, lo_hot = sem("oh_ok"), sem("lo_hot")
        y_out = [sem(f"y_out{n}") for n in range(2)]

        block = es.enter_context(nc.Block())
        XPIECE = 8

        @block.sync
        def _(sp):
            sp.dma_start(posI[:, 0, :], qpos).then_inc(in_p, 16)
            sp.dma_start(posI[:, 1, :], kpos).then_inc(in_p, 16)
            sp.dma_start(srow_f, slope_rows).then_inc(in_p, 16)
            sp.dma_start(brow_f, of_batch).then_inc(in_p, 16)
            for n, w in enumerate((wq, wk, wv, wo)):
                sp.dma_start(wnat[:, n, :], w).then_inc(in_w, 16)
            sp.dma_start(gates[:, 0:1], g_x.unsqueeze(0).broadcast_to([P, 1])).then_inc(in_w, 16)
            sp.dma_start(gates[:, 1:2], g_f.unsqueeze(0).broadcast_to([P, 1])).then_inc(in_w, 16)
            sp.dma_start(bn[:, 0:1], gamma.unsqueeze(1)).then_inc(in_w, 16)
            sp.dma_start(bn[:, 1:2], beta.unsqueeze(1)).then_inc(in_w, 16)
            sp.dma_start(wfn, w_ffn.rearrange("(m p) d -> p m d", p=P)).then_inc(in_w, 16)
            for a in range(2):
                sp.dma_start(keyn[:, a, :, :], keys[4 * a:4 * a + 4].rearrange("h k a d -> (h k) a d")).then_inc(in_w, 16)
            sp.dma_start(kinn, key_in.rearrange("(p l) d -> p l d", l=LO)).then_inc(in_w, 16)
            sp.dma_start(kout, key_out.rearrange("(p l) d -> p l d", l=LO)).then_inc(in_w, 16)
            for n in range(0, T, XPIECE):
                sp.dma_start(X[:, n:n + XPIECE, :], x_t[:, n:n + XPIECE, :]).then_inc(in_x, 16)
            sp.dma_start(maskI, mask_t).then_inc(in_m, 16)
            sp.wait_ge(parts_ok, 1)
            sp.dma_start(krows_d, kparts).then_inc(parts_out, 16)
            for b in range(3):
                sp.dma_start(qrows_d[:, :, b, :], qparts).then_inc(parts_out, 16)
            for par in range(2):
                sp.dma_start(lrow[par][QROWS:ROWS, :], brow_b).then_inc(const_rows, 16)
            sp.wait_ge(parts_out, 64)

            def load(i, j, par):
                wait(sp, in_T, i - 1)
                sp.dma_start(cb[par], ctx_t[i, :, :]).then_inc(ctx_in[par], 16)
                wait(sp, row_tile, 4 * i - 4)
                sp.dma_start(rrow[par][QROWS:ROWS, :], krows_t[i, :, :]).then_inc(rows_in[par], 16)
                sp.dma_start(lrow[par][0:QROWS, :].rearrange("r (c q) -> r c q", c=2), qrows_t[i, :, :, :]).then_inc(rows_in[par], 16)

            steps(sp, load, T)

            def store(p, j, par):
                wait(sp, y_ok, p + 1)
                sp.dma_start(out_t[:, bass.ds(2 * p, 2), :], yb[par]).then_inc(y_out[par], 16)

            steps(sp, store, T // 2)
            for par in range(2):
                sp.wait_ge(y_out[par], 16 * T // 4)

        @block.gpsimd
        def _(pool):
            pool.memset(idf, 0.0).then_inc(ids, 1)
            pool.memset(idb, 0.0).then_inc(ids, 1)
            pool.wait_ge(ids, 2)
            for m in (idf, idb):
                pool.affine_select(out=m, in_=m, compare_op=ALU.not_equal, fill=1.0, base=0,
                                   pattern=[[-1, P]], channel_multiplier=1).then_inc(ids, 1)
            for m in (WqT, WkT, Vb[0], Vb[1]):
                pool.memset(m, 0.0).then_inc(zeros, 1)
            pool.wait_ge(zeros, 4)
            for par in range(2):
                for h2 in range(2):
                    pool.memset(Vb[par][64 * h2:64 * h2 + 64, :, :, h2, HD:HD + 1], 1.0).then_inc(zeros, 1)

            pool.wait_ge(x2_ok, T)
            pool.iota(iota, pattern=[[1, P], [0, HALF]], base=0, channel_multiplier=0,
                      allow_small_or_imprecise_dtypes=True).then_inc(iota_ok, 1)
            pool.iota(iotaL, pattern=[[1, LO], [0, P]], base=0, channel_multiplier=0,
                      allow_small_or_imprecise_dtypes=True).then_inc(iota_ok, 1)
            pool.memset(planes, 0.0).then_inc(iota_ok, 1)
            pool.wait_ge(iota_ok, 3)
            pool.wait_ge(lists_ok, T // G4)

            def lo_hots(p, buf):
                w1s = w1[:, bass.ds(p, 1), :].broadcast_to([P, LO, P])
                w2s = w2[:, bass.ds(p, 1), :].broadcast_to([P, LO, P])
                wait(pool, oh_ok, p + 1)
                wait(pool, p_ps, 4 * (p - 1))
                pool.tensor_tensor(Bm[buf][:, 0], oh, w1s, ALU.mult).then_inc(lo_hot, 1)
                pool.tensor_tensor(Bm[buf][:, 1], oh, w2s, ALU.mult).then_inc(lo_hot, 1)

            def weigh(p, par, gi):
                q, half = gi // 2, gi % 2
                wait(pool, pt_ok, 4 * p + gi + 1)
                wait(pool, gel_sb, 4 * p + 4)
                g = GG[par][:, :, half, HALF * q:HALF * q + HALF]
                pool.tensor_tensor(g, g, Pt[gi % 2], ALU.mult).then_inc(g_ok, 1)

            lo_hots(0, 0)

            def step(p, j, par):
                weigh(p, par, 0)
                weigh(p, par, 1)
                if not (isinstance(p, int) and p == T // 2 - 1):
                    lo_hots(p + 1, 1 - par)
                weigh(p, par, 2)
                weigh(p, par, 3)

            steps(pool, step, T // 2)

        @block.scalar
        def _(act):
            act.wait_ge(in_w, 16 * 13)
            act.activation(gates[:, 2:4], gates[:, 0:2], ACT.Tanh).then_inc(gates_ok, 1)
            act.wait_ge(std_in, 1)
            act.activation(lnt[:, 2, :], lnt[:, 1, :], ACT.Sqrt).then_inc(std_out, 1)

            def inputs_out(i):
                wait(act, in_T, i + 1)
                wait(act, v_ps, i)
                act.activation(xcT.rearrange("p a b -> p (a b)"), PS[:, 0, 0:2 * P], ACT.Copy).then_inc(in_T_sb, 1)

            def q_out(i):
                wait(act, q_ps, i + 1)
                wait(act, row_tile, 4 * i)
                act.activation(Qp.rearrange("p a b -> p (a b)"), PS[:, 1, :], ACT.Copy,
                               scale=float(1.0 / np.sqrt(HD))).then_inc(q_sb, 1)

            def k_out(i):
                wait(act, k_ps, i + 1)
                wait(act, row_tile, 4 * i)
                act.activation(Kp.rearrange("p a b -> p (a b)"), PS[:, 2, :], ACT.Copy).then_inc(k_sb, 1)

            inputs_out(0)
            q_out(0)
            k_out(0)
            inputs_out(1)
            Ef = E.rearrange("p h k -> p (h k)")
            ETf = ET.rearrange("p h k -> p (h k)")

            def step(i, j, par):
                last = isinstance(i, int) and i == T - 1
                if not last:
                    q_out(i + 1)
                for n in range(2):
                    wait(act, shifted, 2 * i + n + 1)
                    act.activation(Ef[:, 512 * n:512 * n + 512], Ef[:, 512 * n:512 * n + 512], ACT.Exp).then_inc(probs, 1)
                if not last:
                    k_out(i + 1)
                wait(act, av_ok, i)
                for n in range(2):
                    wait(act, e_T, 2 * i + n + 1)
                    act.activation(ETf[:, 512 * n:512 * n + 512], PS[:, 5 + n, :], ACT.Copy).then_inc(e_T_sb, 1)
                if not (isinstance(i, int) and i >= T - 2):
                    inputs_out(i + 2)
                if not (isinstance(i, int) and i == 0):
                    attn_out(i - 1)

            def attn_out(i):
                wait(act, attn_T, i + 1)
                wait(act, wo_ok, i)
                act.activation(aT, PS[:, 1, 0:P], ACT.Copy).then_inc(attn_T_sb, 1)

            steps(act, step, T)
            attn_out(T - 1)

            act.wait_ge(std_in, 2)
            act.activation(lnt[:, 2, :], lnt[:, 1, :], ACT.Sqrt).then_inc(std_out, 1)

            def z_out(c, j, par):
                wait(act, z_T, c + 1)
                act.activation(ZT[:, bass.ds(c * 512, 512)], PS[:, par, :], ACT.Copy).then_inc(z_sb, 1)

            steps(act, z_out, T // 4)
            act.wait_ge(std_in, 3)
            act.activation(bn[:, 7:8], bn[:, 4:5], ACT.Sqrt).then_inc(std_out, 1)
            act.wait_ge(bn_ok, 1)
            act.wait_ge(z_sb, T // 4)

            def picks_out(g):
                wait(act, picks_T, g + 1)
                wait(act, lists_ok, g)
                act.activation(codeT.rearrange("p a b -> p (a b)"), PS[:, 2, 0:256], ACT.Copy)
                act.activation(wT.rearrange("p a b -> p (a b)"), PS[:, 2, 256:512], ACT.Copy).then_inc(picks_sb, 1)

            def normed(i, par):
                wait(act, sim_ps, i - 1)
                act.activation(xs[par], ZT[:, bass.ds(i * P, P)], ACT.Identity, bias=bn[:, 6:7],
                               scale=bn[:, 5:6]).then_inc(xs_ok, 1)

            normed(0, 0)

            def select(g, first=False, last=False):
                for k in range(G4):
                    i = G4 * g + k
                    if not (last and k == G4 - 1):
                        normed(i + 1, (k + 1) % 2)
                    wait(act, sim_ps, i + 1)
                    wait(act, sim_used, i - 1)
                    act.activation(sim[k % 2].rearrange("p a h k -> p (a h k)"), PS[:, k % 2, :], ACT.Copy).then_inc(sim_sb, 1)
                wait(act, diff_ok, g + 1)
                act.activation(wgt, wgt, ACT.Exp).then_inc(exp_ok, 1)
                if not first:
                    picks_out(g - 1)

            select(0, first=True)
            select(1)
            with act.Fori(2, T // G4 - 1) as g:
                select(g)
            select(T // G4 - 1, last=True)
            picks_out(T // G4 - 1)

            def second_part(p, gi):
                n = 4 * p + gi
                wait(act, p_ps, n + 1)
                wait(act, pt_ok, n - 1)
                act.activation(p2[gi % 2].rearrange("p l t -> p t l"),
                               PS[:, 2 * (gi % 2):2 * (gi % 2) + 2, :].rearrange("p b (t n) -> p (b t) n", n=16)[:, :, LO:2 * LO],
                               ACT.Copy, scale=1.0 / W2_SCALE).then_inc(p2_sb, 1)

            def gelu(p, par, k):
                m = 4 * p + k
                wait(act, o_ps, m + 1)
                wait(act, f_ps, p - 1)
                act.activation(GG[par][:, 2 * k:2 * k + 2].rearrange("p l h t -> p (l h t)"), PS[:, 4 + k % 2, :],
                               ACT.Gelu).then_inc(gel_sb, 1)

            for k in range(4):
                gelu(0, 0, k)

            def step2(p, j, par):
                more = not (isinstance(p, int) and p == T // 2 - 1)
                second_part(p, 0)
                second_part(p, 1)
                if more:
                    gelu(p + 1, 1 - par, 0)
                    gelu(p + 1, 1 - par, 1)
                second_part(p, 2)
                if more:
                    gelu(p + 1, 1 - par, 2)
                    gelu(p + 1, 1 - par, 3)
                second_part(p, 3)

            steps(act, step2, T // 2)

        @block.tensor
        def _(pe):
            pe.wait_ge(ids, 4)
            pe.wait_ge(in_w, 16 * 13)
            for n in range(4):
                last = pe.transpose(PS[:, 0, n * P:n * P + P], wnat[:, n, :], idf)
            last.then_inc(w_T, 1)
            for n in range(4):
                last = pe.transpose(PS[:, 1, n * P:n * P + P], keyn[:, n // 2, n % 2, :], idf)
            last.then_inc(w_T, 1)
            for n in range(LO):
                last = pe.transpose(PS[:, 2 + n // 4, (n % 4) * P:(n % 4) * P + P], kinn[:, n, :], idf)
            last.then_inc(w_T, 1)
            pe.wait_ge(w_T_sb, 2)
            for a in range(2):
                for h in range(FH):
                    c = (a * FH + h) * NK
                    last = pe.matmul(PS[:, 4, c:c + NK], wfn[:, a * FH + h, :],
                                     keyT[:, h // 4, a, (h % 4) * NK:(h % 4) * NK + NK], start=True, stop=True)
            last.then_inc(w2_ps, 1)
            pe.wait_ge(w2_sb, 1)

            pe.wait_ge(const_rows, 32)
            def inputs_T(i, j, par):
                wait(pe, xn_ready, i + 1)
                wait(pe, ctx_in[par], 16 * (j + 1))
                wait(pe, v_sb, i)
                pe.transpose(PS[:, 0, 0:P], xnb[par], idf)
                pe.transpose(PS[:, 0, P:2 * P], cb[par], idf).then_inc(in_T, 1)

            def project(i):
                wait(pe, in_T_sb, i + 1)
                wait(pe, attn_T_sb, i - 2)
                for g in range(HG):
                    last = pe.matmul(PS[:, 1, g * P:g * P + P], WqT[:, g].rearrange("p a b -> p (a b)"), xcT[:, 0, :],
                                     start=True, stop=True)
                last.then_inc(q_ps, 1)
                wait(pe, x2_ok, i - 2)
                for g in range(HG):
                    last = pe.matmul(PS[:, 2, g * P:g * P + P], WkT[:, g].rearrange("p a b -> p (a b)"), xcT[:, 1, :],
                                     start=True, stop=True)
                last.then_inc(k_ps, 1)
                for b in range(2):
                    for h2 in range(2):
                        last = pe.matmul(PS[64 * h2:64 * h2 + 64, 0, 256 + b * P:256 + b * P + P],
                                         xcT[:, 1, 64 * b:64 * b + 64], WvT, start=True, stop=True)
                last.then_inc(v_ps, 1)

            def scores(i, j, par):
                wait(pe, q_sb, i + 1)
                wait(pe, k_sb, i + 1)
                wait(pe, mask_ok, i + 1)
                wait(pe, rows_in[par], 32 * (j + 1))
                wait(pe, shifted, 2 * i)
                for n in range(2):
                    o = PS[:, 3 + n, :]
                    pe.matmul(o, lrow[par], rrow[par][:, 512 * n:512 * n + 512], start=True, stop=False,
                              skip_group_check=True)
                    pe.matmul(o.rearrange("p (h k) -> p h k", k=S), idb, mb[par].unsqueeze(1).broadcast_to([P, 8, S]),
                              start=False, stop=False, skip_group_check=True)
                for k, r4 in enumerate((0, 2, 1, 3)):
                    if k >= 2:
                        pe.wait_ge(row_tile, 4 * i + k - 1)
                    n, r = r4 // 2, slice(32 * r4, 32 * r4 + HD)
                    for g in range(HG):
                        c = (4 * (r4 % 2) + g) * S
                        for b in range(2):
                            last = pe.matmul(PS[64 * b:64 * b + 64, 3 + n, c:c + S],
                                             Qp[r, g, 64 * b:64 * b + 64], Kp[r, g, 64 * b:64 * b + 64],
                                             start=False, stop=(k >= 2 and g == HG - 1), skip_group_check=True)
                    last.then_inc(row_tile, 1)

            def probs_T(i):
                for n in range(2):
                    wait(pe, probs, 2 * i + n + 1)
                    wait(pe, e_T_sb, 2 * i + n - 1)
                    for c in range(4):
                        p = 4 * n + c
                        last = pe.transpose(PS[:, 5 + n, c * P:c * P + P],
                                            E[:, 2 * p:2 * p + 2, :].rearrange("p h k -> p (h k)"), idf)
                    last.then_inc(e_T, 1)

            def values(i, j, par):
                wait(pe, e_T_sb, 2 * i + 2)
                wait(pe, v_sb, i + 1)
                wait(pe, attn_ok, i)
                for p in range(HP):
                    for b in range(2):
                        last = pe.matmul(PS[64 * b:64 * b + 64, 7, 18 * p:18 * p + 18], ET[:, p, 64 * b:64 * b + 64],
                                         Vb[par][:, b, p].rearrange("p a d -> p (a d)"), start=True, stop=True)
                last.then_inc(av_ok, 1)

            def attn_turn(i):
                wait(pe, attn_ok, i + 1)
                wait(pe, attn_T_sb, i)
                wait(pe, q_sb, min(i + 3, T) if isinstance(i, int) else i + 3)
                pe.transpose(PS[:, 1, 0:P], attn.rearrange("p h d -> p (h d)"), idf).then_inc(attn_T, 1)

            def attn_wo(i):
                wait(pe, attn_T_sb, i + 1)
                wait(pe, x2_ok, i)
                wait(pe, k_sb, min(i + 3, T) if isinstance(i, int) else i + 3)
                pe.matmul(PS[:, 2, 0:P], aT, WoT, start=True, stop=True).then_inc(wo_ok, 1)

            inputs_T(0, 0, 0)
            project(0)
            inputs_T(1, 0, 1)

            def step(i, j, par):
                scores(i, j, par)
                if not (isinstance(i, int) and i == T - 1):
                    project(i + 1)
                probs_T(i)
                if not (isinstance(i, int) and i >= T - 2):
                    inputs_T(i + 2, j + 1, par)
                if not (isinstance(i, int) and i == 0):
                    attn_turn(i - 1)
                values(i, j, par)
                if not (isinstance(i, int) and i == 0):
                    attn_wo(i - 1)

            steps(pe, step, T)
            attn_turn(T - 1)
            attn_wo(T - 1)

            pe.wait_ge(x2_ok, T)

            def z_turn(c, j, par):
                wait(pe, z_ok, c + 1)
                wait(pe, z_sb, c - 1)
                for k in range(4):
                    last = pe.transpose(PS[:, par, k * P:k * P + P], zb[par][:, k, :], idf)
                last.then_inc(z_T, 1)

            steps(pe, z_turn, T // 4)

            pe.wait_ge(z_sb, T // 4)
            pe.wait_ge(z_stat, T // 4)

            def picks_turn(g):
                wait(pe, picks_ok, g + 1)
                wait(pe, picks_sb, g)
                for n, src in enumerate((code, wnorm)):
                    for q in range(2):
                        last = pe.transpose(PS[:, 2, n * 256 + q * P:n * 256 + q * P + P],
                                            src[:, 16 * q:16 * q + 16, :].rearrange("p a b -> p (a b)"), idf)
                last.then_inc(picks_T, 1)

            def sims(g, first=False):
                for k in range(G4):
                    i = G4 * g + k
                    wait(pe, xs_ok, i + 1)
                    wait(pe, sim_sb, i - 1)
                    pe.matmul(PS[:, k % 2, :], xs[k % 2], W2, start=True, stop=True).then_inc(sim_ps, 1)
                if not first:
                    picks_turn(g - 1)

            sims(0, first=True)
            sims(1)
            with pe.Fori(2, T // G4) as g:
                sims(g)
            picks_turn(T // G4 - 1)
            pe.wait_ge(picks_sb, T // G4)

            def expert_in(p, par, k):
                m = 4 * p + k
                wait(pe, gel_sb, m - 1)
                for n in range(2):
                    last = pe.matmul(PS[:, 4 + k % 2, n * 256:n * 256 + 256], kinT[:, 2 * k + n, :],
                                     ZT[:, bass.ds(p * 256, 256)], start=True, stop=True)
                last.then_inc(o_ps, 1)

            def place(p, par, gi):
                q, half = gi // 2, gi % 2
                n = 4 * p + gi
                wait(pe, a_ok, 2 * p + q + 1)
                wait(pe, lo_hot, 2 * p + 2)
                wait(pe, pt_ok, n - 1)
                r = slice(64 * half, 64 * half + 64)
                for t in range(HALF):
                    last = pe.matmul(PS[:, 2 * (gi % 2) + t // 32, 16 * (t % 32):16 * (t % 32) + 16], A[r, q, :, t],
                                     Bm[par][r, :, :, HALF * q + t],
                                     start=True, stop=True)
                last.then_inc(p_ps, 1)

            def expert_out(p, par):
                wait(pe, g_ok, 4 * p + 4)
                wait(pe, y_ok, p)
                for half in range(2):
                    for l in range(LO):
                        last = pe.matmul(PS[:, 6, half * P:half * P + P], GG[par][:, l, half, :], kout[:, l, :],
                                         start=(l == 0), stop=(l == LO - 1))
                last.then_inc(f_ps, 1)

            for k in range(4):
                expert_in(0, 0, k)

            def step2(p, j, par):
                more = not (isinstance(p, int) and p == T // 2 - 1)
                place(p, par, 0)
                place(p, par, 1)
                if not (isinstance(p, int) and p == 0):
                    expert_out(p - 1, 1 - par)
                if more:
                    expert_in(p + 1, 1 - par, 0)
                    expert_in(p + 1, 1 - par, 1)
                place(p, par, 2)
                if more:
                    expert_in(p + 1, 1 - par, 2)
                    expert_in(p + 1, 1 - par, 3)
                place(p, par, 3)

            steps(pe, step2, T // 2)
            expert_out(T // 2 - 1, 1)

        @block.vector
        def _(dve):
            ch = Chain(dve, dve0)

            def layernorm_scale(which, done):
                me, m2e, mo, m2o = (stats[:, :, n] for n in (1, 2, 4, 5))
                ch.add(dve.tensor_tensor(mean, me, mo, ALU.add))
                ch.add(dve.tensor_tensor(lnt[:, 0, :], me, mo, ALU.subtract))
                ch.add(dve.tensor_tensor(lnt[:, 1, :], m2e, m2o, ALU.add))
                ch.settle()
                ch.add(dve.tensor_scalar(mean, mean, 0.5, None, ALU.mult))
                ch.add(dve.tensor_tensor(lnt[:, 0, :], lnt[:, 0, :], lnt[:, 0, :], ALU.mult))
                ch.add(dve.tensor_scalar(lnt[:, 1, :], lnt[:, 1, :], 1.0 / D, EPS, ALU.mult, ALU.add))
                ch.settle()
                dve.scalar_tensor_tensor(lnt[:, 1, :], lnt[:, 0, :], 0.25, lnt[:, 1, :], ALU.mult, ALU.add).then_inc(std_in, 1)
                dve.wait_ge(std_out, done)
                ch.link(dve.reciprocal(rstd, lnt[:, 2, :]))

            dve.wait_ge(in_p, 64)
            ch.link(dve.tensor_copy(posF, posI))
            for h in range(H):
                ch.add(dve.tensor_scalar(kbias[:, h, :], posF[:, 1, :], SLOPES[h], None, ALU.mult))
            for par in range(2):
                ch.add(dve.tensor_copy(rrow[par][0:QROWS, :], srow_f))
            ch.add(dve.tensor_copy(brow_b, brow_f))
            ch.settle()
            kf = kbias.rearrange("p h k -> p (h k)")
            for n in range(3):
                ch.add(dve.tensor_copy(kparts[:, n, :], kf))
                ch.add(dve.tensor_copy(qparts[:, n, :], posF[:, 0, :]))
                ch.settle()
                if n < 2:
                    ch.add(dve.tensor_tensor(kf, kf, kparts[:, n, :], ALU.subtract))
                    ch.add(dve.tensor_tensor(posF[:, 0, :], posF[:, 0, :], qparts[:, n, :], ALU.subtract))
                    ch.settle()
            dve.sem_inc(parts_ok, 1)
            dve.wait_ge(zeros, 8)
            dve.wait_ge(w_T, 1)
            for n, w in enumerate((WqT, WkT)):
                dve.tensor_copy(w[:, :, :, 0:HD], PS[:, 0, n * P:n * P + P].rearrange("p (r g d) -> p g r d", g=HG, r=4))
            dve.tensor_copy(WvT, PS[:, 0, 2 * P:3 * P])
            dve.tensor_copy(WoT, PS[:, 0, 3 * P:4 * P]).then_inc(w_T_sb, 1)
            dve.wait_ge(w_T, 2)
            dve.tensor_copy(keyT.rearrange("p a b k -> p (a b k)"), PS[:, 1, :]).then_inc(w_T_sb, 1)
            dve.wait_ge(w_T, 3)
            dve.tensor_copy(kinT.rearrange("p a b -> p (a b)"), PS[:, 2:4, :].rearrange("p a b -> p (a b)")).then_inc(w_T_sb, 1)
            dve.wait_ge(gates_ok, 1)
            ch.add(dve.tensor_scalar(gates[:, 3:4], gates[:, 3:4], 1.0 / W_SCALE, None, ALU.mult))
            dve.wait_ge(w2_ps, 1)
            dve.tensor_copy(W2, PS[:, 4, :]).then_inc(w2_sb, 1)
            dve.wait_ge(in_x, 16 * T // XPIECE)
            with dve.Fori(0, T // 2) as j:
                for par in range(2):
                    dve.bn_stats(stats[:, bass.ds(2 * j + par, 1), :], X[:, bass.ds(2 * j + par, 1), :]).then_inc(stat_ok, 1)
            dve.wait_ge(stat_ok, T)
            layernorm_scale(0, 1)

            dve.wait_ge(in_m, 16)

            def normalise(i, par):
                wait(dve, in_T, i - 1)
                dve.tensor_scalar(xnb[par].unsqueeze(1), X[:, bass.ds(i, 1), :], mean[:, bass.ds(i, 1)], rstd[:, bass.ds(i, 1)],
                                  ALU.subtract, ALU.mult).then_inc(xn_ready, 1)

            def mask_term(i, par):
                wait(dve, row_tile, 4 * i - 4)
                dve.tensor_scalar(mb[par].unsqueeze(1), maskI[:, bass.ds(i, 1), :], 0.0, MASKED, ALU.is_equal,
                                  ALU.mult).then_inc(mask_ok, 1)

            def v_out(i, par):
                wait(dve, v_ps, i + 1)
                wait(dve, av_ok, i - 1)
                for h2 in range(2):
                    r = slice(64 * h2, 64 * h2 + 64)
                    src = PS[r, 0, 256:512].rearrange("p (b h a d) -> p b h a d", b=2, h=HP, a=2)
                    last = dve.tensor_copy(Vb[par][r, :, :, h2, 0:HD], src[:, :, :, h2, :])
                last.then_inc(v_sb, 1)

            def residual(i):
                wait(dve, wo_ok, i + 1)
                xi = X[:, bass.ds(i, 1), :]
                dve.scalar_tensor_tensor(xi, PS[:, 2, 0:P].unsqueeze(1), gates[:, 2:3], xi, ALU.mult,
                                         ALU.add).then_inc(x2_ok, 1)
                wait(dve, x2_ok, i + 1)
                dve.bn_stats(stats[:, bass.ds(i, 1), :], xi).then_inc(stat_ok, 1)

            normalise(0, 0)
            normalise(1, 1)
            mask_term(0, 0)
            v_out(0, 0)
            LINKS = 3
            link1 = Chain(dve, dve1)

            def step(i, j, par):
                link1.at(LINKS * i)
                wait(dve, row_tile, 4 * i + 4)
                s = PS[:, 3:5, :].rearrange("p b (h k) -> p (b h) k", k=S)
                link1.link(dve.tensor_reduce(smax, s, AX.X, ALU.max))
                wait(dve, e_T, 2 * i)
                for n in range(2):
                    hs = slice(8 * n, 8 * n + 8)
                    dve.tensor_tensor(E[:, hs, :], s[:, hs, :], rows(smax[:, hs], S), ALU.subtract).then_inc(shifted, 1)
                if not (isinstance(i, int) and i == T - 1):
                    mask_term(i + 1, 1 - par)
                    v_out(i + 1, 1 - par)
                if not (isinstance(i, int) and i >= T - 2):
                    normalise(i + 2, par)
                wait(dve, av_ok, i + 1)
                o = PS[:, 7, 0:144].rearrange("p (h e) -> p h e", e=HD + 1)
                link1.link(dve.tensor_scalar(den, o[:, :, HD], 1.0, None, ALU.add))
                link1.link(dve.reciprocal(den, den))
                wait(dve, attn_T, i)
                dve.tensor_tensor(attn, o[:, :, 0:HD], rows(den, HD), ALU.mult).then_inc(attn_ok, 1)
                assert link1.n == LINKS
                if not (isinstance(i, int) and i == 0):
                    residual(i - 1)

            steps(dve, step, T)
            residual(T - 1)

            dve.wait_ge(stat_ok, 2 * T)
            layernorm_scale(1, 2)

            def normalise2(c, par):
                wait(dve, z_T, c - 1)
                for k in range(4):
                    i = 4 * c + k
                    last = dve.tensor_scalar(zb[par][:, k:k + 1, :], X[:, bass.ds(i, 1), :], mean[:, bass.ds(i, 1)],
                                             rstd[:, bass.ds(i, 1)], ALU.subtract, ALU.mult)
                last.then_inc(z_ok, 1)

            normalise2(0, 0)

            def step1b(c, j, par):
                if not (isinstance(c, int) and c == T // 4 - 1):
                    normalise2(c + 1, 1 - par)
                wait(dve, z_sb, c + 1)
                dve.bn_stats(stats[:, bass.ds(c, 1), :], ZT[:, bass.ds(c * 512, 512)]).then_inc(z_stat, 1)

            steps(dve, step1b, T // 4)
            dve.wait_ge(z_stat, T // 4)
            ch.link(dve.bn_aggr(bn[:, 2:4], stats[:, 0:T // 4, :].rearrange("p a b -> p (a b)")))
            dve.tensor_scalar(bn[:, 4:5], bn[:, 3:4], EPS, None, ALU.add).then_inc(std_in, 1)
            dve.wait_ge(std_out, 3)
            ch.link(dve.reciprocal(bn[:, 4:5], bn[:, 7:8]))
            ch.link(dve.tensor_tensor(bn[:, 5:6], bn[:, 4:5], bn[:, 0:1], ALU.mult))
            ch.link(dve.tensor_tensor(bn[:, 7:8], bn[:, 5:6], bn[:, 2:3], ALU.mult))
            dve.tensor_tensor(bn[:, 6:7], bn[:, 1:2], bn[:, 7:8], ALU.subtract).then_inc(bn_ok, 1)

            dve.wait_ge(iota_ok, 3)
            LINKS2 = 4 * 4 + 9
            link2 = Chain(dve, dve2)

            def lists(g):
                wait(dve, picks_sb, g + 1)
                link2.add(dve.tensor_scalar(codeHL[:, 0], codeT, 3, None, ALU.logical_shift_right))
                link2.add(dve.tensor_scalar(codeHL[:, 1], codeT, 7, None, ALU.bitwise_and))
                here = bass.ds(2 * g, 2)
                link2.add(dve.tensor_scalar(w1[:, here, :], wT, W_SCALE, None, ALU.mult))
                link2.settle()
                dve.tensor_copy(hi16[:, here, :], codeHL[:, 0])
                dve.tensor_copy(lo16[:, here, :], codeHL[:, 1])
                link2.link(dve.scalar_tensor_tensor(wRest, wT, W_SCALE, w1[:, here, :], ALU.mult, ALU.subtract))
                dve.tensor_scalar(w2[:, here, :], wRest, W2_SCALE, None, ALU.mult).then_inc(lists_ok, 1)

            def select(g, first=False):
                for k in range(G4):
                    i = G4 * g + k
                    par = k % 2
                    wait(dve, sim_sb, i + 1)
                    dve.nop(nofuse=True)
                    for a in range(2):
                        for h in range(FH):
                            last = dve.max(s8[par][:, a, h, :], sim[par][:, a, h, :])
                    link2.link(last)
                    link2.add(dve.tensor_tensor(cand[par], rows(s8[par][:, 0], K8),
                                                s8[par][:, 1].unsqueeze(2).broadcast_to([P, FH, K8, K8]), ALU.add))
                    for a in range(2):
                        for h in range(FH):
                            last = dve.max_index(i8[:, a, k * FH + h, :], s8[par][:, a, h, :], sim[par][:, a, h, :])
                    last.then_inc(sim_used, 1)
                    link2.settle()
                    dve.nop(nofuse=True)
                    for h in range(FH):
                        last = dve.max(val[:, k * FH + h, :], cand[par][:, h].rearrange("p a b -> p (a b)"))
                    link2.link(last)
                    dve.nop(nofuse=True)
                    for h in range(FH):
                        last = dve.max_index(pk[:, k * FH + h, :], val[:, k * FH + h, :],
                                             cand[par][:, h].rearrange("p a b -> p (a b)"))
                    link2.add(last)
                dve.tensor_tensor(wgt, val, rows(val[:, :, 0], K8), ALU.subtract).then_inc(diff_ok, 1)
                link2.settle()
                dve.wait_ge(sim_used, G4 * g + G4)
                dve.tensor_scalar(pab[:, 0], pk, 3, None, ALU.logical_shift_right)
                dve.tensor_scalar(pab[:, 1], pk, 7, None, ALU.bitwise_and)
                dve.tensor_scalar(i8f[:, 0], i8[:, 0], float(NK), None, ALU.mult)
                link2.link(dve.tensor_copy(i8f[:, 1], i8[:, 1]))
                for n in range(2):
                    for a in range(K8):
                        last = dve.scalar_tensor_tensor(planes[:, n * K8 + a, :, a:K8], pab[:, n, :, a:K8], float(a),
                                                        rows(i8f[:, n, :, a], K8 - a), ALU.is_equal, ALU.mult)
                link2.link(last)
                pf = planes.rearrange("p n h k -> p n (h k)")
                tf = tree.rearrange("p n h k -> p n (h k)")
                link2.link(dve.tensor_tensor(tf, pf[:, 0:8], pf[:, 8:16], ALU.add))
                link2.link(dve.tensor_tensor(tf[:, 0:4], tf[:, 0:4], tf[:, 4:8], ALU.add))
                link2.link(dve.tensor_tensor(tf[:, 0:2], tf[:, 0:2], tf[:, 2:4], ALU.add))
                wait(dve, picks_T, g)
                dve.tensor_tensor(code.rearrange("p h k -> p (h k)"), tf[:, 0], tf[:, 1], ALU.add)
                wait(dve, exp_ok, g + 1)
                link2.link(dve.tensor_reduce(wsum, wgt, AX.X, ALU.add))
                link2.link(dve.reciprocal(wsum, wsum))
                dve.tensor_tensor(wnorm, wgt, rows(wsum, K8), ALU.mult).then_inc(picks_ok, 1)
                if not first:
                    lists(g - 1)

            FIRST, EACH, LAST = 4 * 3 + 4 * 1 + 7, 4 * 3 + 4 * 1 + 7 + 4, 4
            link2.at(0)
            select(0, first=True)
            assert link2.n == FIRST, link2.n
            with dve.Fori(1, T // G4) as g:
                link2.at(FIRST + (g - 1) * EACH)
                select(g)
                assert link2.n == EACH, link2.n
            link2.at(FIRST + (T // G4 - 1) * EACH)
            lists(T // G4 - 1)
            dve.wait_ge(lists_ok, T // G4)

            def hi_hots(p, q):
                wait(dve, p_ps, 4 * p + 2 * q - 2)
                src = hi16[:, bass.ds(p, 1), HALF * q:HALF * q + HALF]
                for n in range(2):
                    v = slice(64 * n, 64 * n + 64)
                    last = dve.tensor_tensor(A[:, q, v, :], src.broadcast_to([P, 64, HALF]), iota[:, v, :], ALU.is_equal)
                last.then_inc(a_ok, 1)

            def joined(p, gi):
                n = 4 * p + gi
                wait(dve, p2_sb, n + 1)
                wait(dve, g_ok, n - 1)
                first = PS[:, 2 * (gi % 2):2 * (gi % 2) + 2, :].rearrange("p b (t n) -> p (b t) n", n=16)[:, :, 0:LO]
                dve.tensor_tensor(Pt[gi % 2], first.rearrange("p t l -> p l t"), p2[gi % 2], ALU.add).then_inc(pt_ok, 1)

            def finish(p, j, par):
                wait(dve, f_ps, p + 1)
                wait(dve, y_out[par], 16 * j)
                dve.scalar_tensor_tensor(yb[par], PS[:, 6, 0:256].rearrange("p (a d) -> p a d", a=2), gates[:, 3:4],
                                         X[:, bass.ds(2 * p, 2), :], ALU.mult, ALU.add).then_inc(y_ok, 1)

            def lo_ones(p):
                wait(dve, lo_hot, 2 * p)
                dve.tensor_tensor(oh, lo16[:, bass.ds(p, 1), :].broadcast_to([P, LO, P]), iotaL,
                                  ALU.is_equal).then_inc(oh_ok, 1)

            lo_ones(0)
            hi_hots(0, 0)
            hi_hots(0, 1)

            def step2(p, j, par):
                more = not (isinstance(p, int) and p == T // 2 - 1)
                joined(p, 0)
                joined(p, 1)
                if more:
                    lo_ones(p + 1)
                    hi_hots(p + 1, 0)
                if not (isinstance(p, int) and p == 0):
                    finish(p - 1, j if par else j - 1, 1 - par)
                joined(p, 2)
                joined(p, 3)
                if more:
                    hi_hots(p + 1, 1)

            steps(dve, step2, T // 2, lead=4)
            finish(T // 2 - 1, T // 4 - 1, 1)


_INS = ["x", "ctx_1024", "itok_BxS_8_8191", "itok_BxS2_1_8191", "mask_BxSxS2_if1", "g_xattn", "g_ffn", "L0_xattn_W_q",
        "L0_xattn_W_k", "L0_xattn_W_v", "L0_xattn_W_o", "L0_ffn_gamma", "L0_ffn_beta", "L0_ffn_w_q", "L0_ffn_keys",
        "L0_ffn_key_in", "L0_ffn_key_out"]


def kernel(**inputs):
    import concourse.bacc as bacc
    from concourse.bass_utils import run_bass_kernel_spmd

    nc = bacc.Bacc("TRN2", target_bir_lowering=False, num_devices=1)
    arrays, args = {}, []
    given = [(n, inputs[n]) for n in _INS] + list(zip(("slope_rows", "of_batch"), shape_constants()))
    for name, a in given:
        a = np.ascontiguousarray(a)
        arrays[f"in_{name}"] = a
        args.append(nc.dram_tensor(f"in_{name}", a.shape, mybir.dt.from_np(a.dtype), kind="ExternalInput").ap())
    args.append(nc.dram_tensor("out_0", (B, S, D), F32, kind="ExternalOutput").ap())
    gated_block(nc, *args)
    r = run_bass_kernel_spmd(nc, [arrays], core_ids=[0])
    return r.results[0]["out_0"]
```

```python
import concourse.bass as bass
from concourse import mybir
from contextlib import ExitStack
import numpy as np

F32 = mybir.dt.float32
BF16 = mybir.dt.bfloat16
F16 = mybir.dt.float16
I32 = mybir.dt.int32
U16 = mybir.dt.uint16
ALU = mybir.AluOpType
ACT = mybir.ActivationFunctionType
AX = mybir.AxisListType

P = 128
B, S, D = 128, 64, 128
T = B * S // P
H, HD = 16, 8
HG = H // 4
HP = H // 2
XPIECE = 8
FH, NK, K8 = 8, 32, 8
LO = NK * NK // P
QROWS, KROWS = 9, 6
ROWS = QROWS + KROWS
G4 = 4
PAIRS = [(a, b) for a in range(K8) for b in range(K8) if (a + 1) * (b + 1) <= K8]
NC = len(PAIRS)
BLOCKS = [(0, slice(0, 1), slice(0, 8)), (8, slice(1, 2), slice(0, 4)), (12, slice(2, 4), slice(0, 2)),
          (16, slice(4, 8), slice(0, 1))]
HALF = P // 2
Q32 = P // 4
MASKED = -1.0e30
EPS = 1e-5
W_SCALE = 2.0 ** 14
W2_SCALE = 2.0 ** 11
QK_SCALE = 2.0 ** 4
SCORE = QK_SCALE ** 2
SLOPES = [float(np.float32((2.0 ** (-8.0 / H)) ** i)) for i in range(1, H + 1)]


def bf16_parts(v):
    out, rest = [], np.asarray(v, np.float32)
    for _ in range(3):
        top = (rest.view(np.uint32) & np.uint32(0xFFFF0000)).view(np.float32)
        out.append(top)
        rest = rest - top
    return out


def shape_constants():
    s = bf16_parts(-np.asarray(SLOPES, np.float32) * np.float32(SCORE))
    slope_rows = np.stack([np.repeat(s[j], S) for _ in range(3) for j in range(3)])
    of_batch = np.zeros((KROWS, P), np.float32)
    of_batch[0:3, 0:S] = 1.0
    of_batch[3:6, S:P] = 1.0
    copy = (np.arange(P) // HD) % 4
    low = -np.stack([copy >= 2, copy % 2 == 1], 1).astype(np.float32)
    return np.ascontiguousarray(slope_rows, np.float32), of_batch, np.ascontiguousarray(low)


def wait(eng, sem, value):
    if not (isinstance(value, int) and value <= 0):
        eng.wait_ge(sem, value)


def steps(eng, body, n, lead=2, tail=2):
    for i in range(lead):
        body(i, i // 2, i % 2)
    with eng.Fori(lead // 2, (n - tail) // 2) as j:
        for par in range(2):
            body(2 * j + par, j, par)
    for i in range(n - tail, n):
        body(i, i // 2, i % 2)


class Chain:

    def __init__(self, eng, sem, start=0):
        self.eng, self.sem, self.base, self.n = eng, sem, start, 0

    def at(self, base):
        self.base, self.n = base, 0

    def add(self, ins):
        self.n += 1
        ins.then_inc(self.sem, 1)

    def settle(self, but=0):
        wait(self.eng, self.sem, self.base + self.n - but)

    def link(self, ins):
        self.add(ins)
        self.settle()


def rows(ap, count):
    s = list(ap.shape)
    return ap.unsqueeze(len(s)).broadcast_to(s + [count])


def gated_block(nc, x, ctx, qpos, kpos, mask, g_x, g_f, wq, wk, wv, wo, gamma, beta, w_ffn, keys,
                key_in, key_out, slope_rows, of_batch, low_rows, out):
    x_t = x.rearrange("(i c) s d -> (c s) i d", c=2)
    ctx_t = ctx.rearrange("(i c) s d -> i (c s) d", c=2)
    mask_t = mask.rearrange("(i c) q k -> (c q) i k", c=2)
    out_t = out.rearrange("(i c) s d -> (c s) i d", c=2)
    krows_d = nc.dram_tensor("krows_d", (B, 3, H * S), BF16, kind="Internal").ap()
    qrows_d = nc.dram_tensor("qrows_d", (B, 3, 3, S), BF16, kind="Internal").ap()
    krows_t = krows_d.rearrange("(i c) p n -> i (c p) n", c=2)
    qrows_t = qrows_d.rearrange("(i c) a b q -> i (a b) c q", c=2)

    es = ExitStack()
    with es:
        def sb(name, shape, dt=F32):
            return es.enter_context(nc.sbuf_tensor(name, shape, dt))[:]

        def sem(name):
            return es.enter_context(nc.semaphore(name))

        X = sb("X", [P, T, D])
        ZT = sb("ZT", [P, T * P])
        idf = sb("idf", [P, P])
        idb = sb("idb", [P, P], BF16)
        idh = sb("idh", [P, P], F16)
        stats = sb("stats", [P, T, 6])
        lnt = sb("lnt", [P, 3, T])
        mean = sb("mean", [P, T])
        rstd = sb("rstd", [P, T])
        W2 = sb("W2", [P, 2 * FH * NK])
        kinT = sb("kinT", [P, LO, P])
        kout = sb("kout", [P, LO, D])
        low = sb("low", [P, 2])
        gates = sb("gates", [P, 4])
        bn = sb("bn", [P, 8])
        A = sb("A", [P, 2, P, HALF], F16)
        WORDS = 24576
        AR = sb("AR", [P, WORDS])

        def carver(area, total, start=0):
            at = [start]

            def carve(shape, dt=F32):
                n = int(np.prod(shape[1:]))
                words = n if dt in (F32, I32) else (n + 1) // 2
                v = area[0:shape[0], at[0]:at[0] + words]
                at[0] += (words + 7) // 8 * 8
                assert at[0] <= total, at[0]
                if dt != F32:
                    v = v.bitcast(dt)
                if len(shape) > 2:
                    names = "abcd"[:len(shape) - 1]
                    v = v.rearrange(f"p ({' '.join(names)}) -> p {' '.join(names)}",
                                    **{c: shape[1 + q] for q, c in enumerate(names)})
                return v
            return carve, at

        carve, _ = carver(AR, WORDS)
        WqT = carve([P, HG, 4, 4, HD])
        WkT = carve([P, HG, 4, 4, HD])
        WvT = carve([P, D])
        WoT = carve([P, D])
        maskI = carve([P, T, S], I32)
        cb = [carve([P, D]) for _ in range(2)]
        xnb = [carve([P, D]) for _ in range(2)]
        lrow = [carve([ROWS, P], BF16) for _ in range(2)]
        rrow = [carve([ROWS, H * S], BF16) for _ in range(2)]
        mb = [carve([P, S], BF16) for _ in range(2)]
        xT = carve([P, P])
        cT = carve([P, 2, 2, S])
        Qp = carve([P, HG, P], F16)
        Kp = carve([P, HG, P], F16)
        Vb = [carve([P, 2, HP, 2, HD + 1]) for _ in range(2)]
        E = carve([P, H, S])
        ET = carve([P, HP, P])
        smax = carve([P, H])
        den = carve([P, H])
        attn = carve([P, H, HD])
        aT = carve([P, P])
        zcarve, _ = carver(ZT, T * P)
        wnat = zcarve([P, 4, D])
        wfn = A.rearrange("p a v t -> p (a v t)").bitcast(F32)[:, 0:2 * FH * D].rearrange("p (m d) -> p m d", d=D)
        keyn = zcarve([P, 2, 2, D])
        keyT = zcarve([P, 2, 2, P])
        kinn = zcarve([P, LO, D])
        posI = zcarve([P, 2, S], I32)
        posF = zcarve([P, 2, S])
        kbias = zcarve([P, H, S])
        kparts = zcarve([P, 3, H * S], BF16)
        qparts = zcarve([P, 3, S], BF16)
        srow_f = zcarve([QROWS, H * S])
        brow_f = zcarve([KROWS, P])
        brow_b = zcarve([KROWS, P], BF16)
        carve, at = carver(AR, WORDS)
        iota = carve([P, P, HALF], F16)
        iotaL = carve([P, LO, P], F16)
        hi16 = carve([P, T // 2, P], F16)
        lo16 = carve([P, T // 2, P], F16)
        w1 = carve([P, T // 2, P], F16)
        w2 = carve([P, T // 2, P], F16)
        shared = at[0]
        zb = [carve([P, 4, D]) for _ in range(2)]
        xs = [carve([P, P]) for _ in range(2)]
        sim = [carve([P, 2, FH, NK]) for _ in range(2)]
        s8 = [carve([P, 2, FH, K8]) for _ in range(2)]
        i8 = carve([P, 2, G4 * FH, K8], U16)
        i8f = carve([P, 2, G4 * FH, K8], F16)
        cand = [carve([P, FH, NC]) for _ in range(2)]
        ccode = carve([P, G4 * FH, NC], F16)
        val = carve([P, G4 * FH, K8])
        pk = carve([P, G4 * FH, K8], U16)
        planes = carve([P, NC, G4 * FH, K8], F16)
        wgt = carve([P, G4 * FH, K8])
        wnorm = carve([P, G4 * FH, K8])
        wsum = carve([P, G4 * FH])
        codeT = carve([P, 2, P], U16)
        codeHL = carve([P, 2, 2, P], U16)
        wRest = carve([P, 2, P])
        wFull = carve([P, 2, P])
        carve, at = carver(AR, WORDS, shared)
        Bm = [carve([P, 2, 2, LO, P], F16) for _ in range(2)]
        oh = carve([P, 2, LO, P], F16)
        GG = [carve([P, LO, 2, P]) for _ in range(2)]
        p2 = [carve([P, LO, 2, Q32]) for _ in range(2)]
        Pt = [carve([P, LO, 2, Q32]) for _ in range(2)]
        yb = [carve([P, 2, D]) for _ in range(2)]

        PS = es.enter_context(nc.psum_tensor("PS", [P, 8, 512], F32))[:]

        in_w, in_p = sem("in_w"), sem("in_p")
        in_m = [sem(f"in_m{n}") for n in range(2)]
        in_x = [sem(f"in_x{n}") for n in range(T // XPIECE)]
        ids, zeros, const_rows, prep = sem("ids"), sem("zeros"), sem("const_rows"), sem("prep")
        w_T, w_T_sb, w2_ps, w2_sb, gates_ok = (sem(n) for n in ("w_T", "w_T_sb", "w2_ps", "w2_sb", "gates_ok"))
        parts_ok, parts_out, std_in, std_out = (sem(n) for n in ("parts_ok", "parts_out", "std_in", "std_out"))
        ctx_in = [sem(f"ctx_in{n}") for n in range(2)]
        rows_in = [sem(f"rows_in{n}") for n in range(2)]
        xn_ready, in_T, in_T_sb = sem("xn_ready"), sem("in_T"), sem("in_T_sb")
        q_ps, k_ps, v_ps, q_hi, k_hi, q_sb, k_sb, v_sb = (
            sem(n) for n in ("q_ps", "k_ps", "v_ps", "q_hi", "k_hi", "q_sb", "k_sb", "v_sb"))
        mask_ok, shifted, probs = (sem(n) for n in ("mask_ok", "shifted", "probs"))
        e_T, e_T_sb, av_ok, attn_ok = (sem(n) for n in ("e_T", "e_T_sb", "av_ok", "attn_ok"))
        attn_T, attn_T_sb, wo_ok, x2_ok, stat_ok = (
            sem(n) for n in ("attn_T", "attn_T_sb", "wo_ok", "x2_ok", "stat_ok"))
        dve0, dve1, dve2 = (sem(f"dve{n}") for n in range(3))
        z_ok, z_T, z_sb, z_stat, bn_ok = (sem(n) for n in ("z_ok", "z_T", "z_sb", "z_stat", "bn_ok"))
        xs_ok, sim_ps, sim_sb = (sem(n) for n in ("xs_ok", "sim_ps", "sim_sb"))
        idx_ok, val_ok, ccode_ok, planes_ok, diff_ok, exp_ok, rsum_ok = (
            sem(n) for n in ("idx_ok", "val_ok", "ccode_ok", "planes_ok", "diff_ok", "exp_ok", "rsum_ok"))
        picks_ok, picks_T, picks_sb, split_ok, hl_ok, w_ok, rest_ok, oh_zero = (
            sem(n) for n in ("picks_ok", "picks_T", "picks_sb", "split_ok", "hl_ok", "w_ok", "rest_ok", "oh_zero"))
        iota_ok = sem("iota_ok")
        picks_hot = sem("picks_hot")
        z_act, shift_ok = sem("z_act"), sem("shift_ok")
        a_ok, p_ps, p2_sb, pt_ok, g_ok = (sem(n) for n in ("a_ok", "p_ps", "p2_sb", "pt_ok", "g_ok"))
        o_ps, gel_sb, f_ps, y_ok = (sem(n) for n in ("o_ps", "gel_sb", "f_ps", "y_ok"))
        row_tile, poolc = sem("row_tile"), sem("poolc")
        oh_ok, lo_hot = sem("oh_ok"), sem("lo_hot")
        y_out = [sem(f"y_out{n}") for n in range(2)]

        def placed(gi, part):
            two = PS[:, 2 * (gi % 2):2 * (gi % 2) + 2, :].rearrange("p b n -> p (b n)")
            return two.rearrange("p (t a c l) -> p l a c t", a=2, c=2, l=LO)[:, :, :, part, :]

        block = es.enter_context(nc.Block())

        @block.sync
        def _(sp):
            sp.dma_start(posI[:, 0, :], qpos).then_inc(in_p, 16)
            sp.dma_start(posI[:, 1, :], kpos).then_inc(in_p, 16)
            sp.dma_start(srow_f, slope_rows).then_inc(in_p, 16)
            sp.dma_start(brow_f, of_batch).then_inc(in_p, 16)
            sp.dma_start(low, low_rows).then_inc(in_p, 16)
            for n, w in enumerate((wq, wk, wv, wo)):
                sp.dma_start(wnat[:, n, :], w).then_inc(in_w, 16)
            sp.dma_start(gates[:, 0:1], g_x.unsqueeze(0).broadcast_to([P, 1])).then_inc(in_w, 16)
            sp.dma_start(gates[:, 1:2], g_f.unsqueeze(0).broadcast_to([P, 1])).then_inc(in_w, 16)
            sp.dma_start(bn[:, 0:1], gamma.unsqueeze(1)).then_inc(in_w, 16)
            sp.dma_start(bn[:, 1:2], beta.unsqueeze(1)).then_inc(in_w, 16)
            sp.dma_start(wfn, w_ffn.rearrange("(m p) d -> p m d", p=P)).then_inc(in_w, 16)
            for a in range(2):
                sp.dma_start(keyn[:, a, :, :], keys[4 * a:4 * a + 4].rearrange("h k a d -> (h k) a d")).then_inc(in_w, 16)
            sp.dma_start(kinn, key_in.rearrange("(p l) d -> p l d", l=LO)).then_inc(in_w, 16)
            sp.dma_start(kout, key_out.rearrange("(p l) d -> p l d", l=LO)).then_inc(in_w, 16)
            for n in range(0, T, XPIECE):
                sp.dma_start(X[:, n:n + XPIECE, :], x_t[:, n:n + XPIECE, :]).then_inc(in_x[n // XPIECE], 16)
            sp.dma_start(maskI[:, 0:XPIECE, :], mask_t[:, 0:XPIECE, :]).then_inc(in_m[0], 16)
            sp.wait_ge(parts_ok, 1)
            sp.dma_start(krows_d, kparts).then_inc(parts_out, 16)
            for b in range(3):
                sp.dma_start(qrows_d[:, :, b, :], qparts).then_inc(parts_out, 16)
            for par in range(2):
                sp.dma_start(lrow[par][QROWS:ROWS, :], brow_b).then_inc(const_rows, 16)
            sp.wait_ge(parts_out, 64)

            def load(i, j, par):
                wait(sp, in_T, i - 1)
                sp.dma_start(cb[par], ctx_t[i, :, :]).then_inc(ctx_in[par], 16)
                wait(sp, row_tile, 4 * i - 4)
                sp.dma_start(rrow[par][QROWS:ROWS, :], krows_t[i, :, :]).then_inc(rows_in[par], 16)
                sp.dma_start(lrow[par][0:QROWS, :].rearrange("r (c q) -> r c q", c=2), qrows_t[i, :, :, :]).then_inc(rows_in[par], 16)

            load(0, 0, 0)
            load(1, 0, 1)
            sp.dma_start(maskI[:, XPIECE:, :], mask_t[:, XPIECE:, :]).then_inc(in_m[1], 16)
            with sp.Fori(1, T // 2) as j:
                for par in range(2):
                    load(2 * j + par, j, par)

            def store(p, j, par):
                wait(sp, y_ok, p + 1)
                sp.dma_start(out_t[:, bass.ds(2 * p, 2), :], yb[par]).then_inc(y_out[par], 16)

            steps(sp, store, T // 2)
            for par in range(2):
                sp.wait_ge(y_out[par], 16 * T // 4)

        @block.gpsimd
        def _(pool):
            pool.memset(idf, 0.0).then_inc(ids, 1)
            pool.memset(idb, 0.0).then_inc(ids, 1)
            pool.memset(idh, 0.0).then_inc(ids, 1)
            pool.wait_ge(ids, 3)
            for m in (idf, idb, idh):
                pool.affine_select(out=m, in_=m, compare_op=ALU.not_equal, fill=1.0, base=0,
                                   pattern=[[-1, P]], channel_multiplier=1).then_inc(ids, 1)
            for m in Vb:
                pool.memset(m, 0.0).then_inc(zeros, 1)
            pool.wait_ge(zeros, 2)
            for par in range(2):
                for h2 in range(2):
                    pool.memset(Vb[par][64 * h2:64 * h2 + 64, :, :, h2, HD:HD + 1], 1.0).then_inc(zeros, 1)

            pool.wait_ge(x2_ok, T)
            pool.iota(iota, pattern=[[1, P], [0, HALF]], base=0, channel_multiplier=0,
                      allow_small_or_imprecise_dtypes=True).then_inc(iota_ok, 1)
            pool.iota(iotaL, pattern=[[1, LO], [0, P]], base=0, channel_multiplier=0,
                      allow_small_or_imprecise_dtypes=True).then_inc(iota_ok, 1)
            pool.memset(planes, 0.0).then_inc(iota_ok, 1)
            pool.wait_ge(iota_ok, 3)

            def weight_rest(g):
                wait(pool, picks_sb, g + 1)
                pool.nop(nofuse=True)
                pool.tensor_tensor(wRest, wFull, w1[:, bass.ds(2 * g, 2), :], ALU.subtract).then_inc(rest_ok, 1)

            def candidates(g, first=False):
                if not first:
                    weight_rest(g - 1)
                wait(pool, idx_ok, G4 * g + G4)
                pool.nop(nofuse=True)
                pool.tensor_scalar(i8f[:, 0], i8[:, 0], float(NK), 1.0, ALU.mult, ALU.mult).then_inc(poolc, 1)
                pool.tensor_copy(i8f[:, 1], i8[:, 1]).then_inc(poolc, 1)
                wait(pool, poolc, 2 * g + 2)
                wait(pool, planes_ok, g)
                for at, ra, rb in BLOCKS:
                    na, nb = ra.stop - ra.start, rb.stop - rb.start
                    last = pool.tensor_tensor(ccode[:, :, at:at + na * nb].rearrange("p t (a b) -> p t a b", a=na),
                                              rows(i8f[:, 0, :, ra], nb),
                                              i8f[:, 1, :, rb].unsqueeze(2).broadcast_to([P, G4 * FH, na, nb]), ALU.add)
                last.then_inc(ccode_ok, 1)
                wait(pool, val_ok, g + 1)
                wait(pool, picks_ok, g)
                pool.tensor_tensor(wgt, val, rows(val[:, :, 0], K8), ALU.subtract).then_inc(diff_ok, 1)
                wait(pool, picks_hot, g + 1)
                wait(pool, ccode_ok, g + 1)
                pool.nop(nofuse=True)
                for c, (a, b) in enumerate(PAIRS):
                    k0 = (a + 1) * (b + 1) - 1
                    last = pool.tensor_tensor(planes[:, c, :, k0:K8], planes[:, c, :, k0:K8],
                                              rows(ccode[:, :, c], K8 - k0), ALU.mult)
                last.then_inc(planes_ok, 1)
                wait(pool, rsum_ok, g + 1)
                wait(pool, picks_T, g)
                pool.tensor_tensor(wnorm, wgt, rows(wsum, K8), ALU.mult).then_inc(picks_ok, 1)

            candidates(0, first=True)
            candidates(1)
            with pool.Fori(2, T // G4) as g:
                candidates(g)
            weight_rest(T // G4 - 1)
            pool.wait_ge(picks_T, T // G4)
            pool.wait_ge(split_ok, T // G4)
            pool.wait_ge(hl_ok, T // G4)
            pool.wait_ge(w_ok, T // G4)
            pool.memset(oh, 0.0).then_inc(oh_zero, 1)

            def lo_hots(p, buf, q):
                wait(pool, oh_ok, p + 1)
                wait(pool, p_ps, 4 * p + 2 * q - 6)
                pool.nop(nofuse=True)
                toks = slice(HALF * q, HALF * q + HALF)
                for part, w in enumerate((w1, w2)):
                    last = pool.tensor_tensor(Bm[buf][:, :, part, :, toks], oh[:, :, :, toks],
                                              w[:, bass.ds(p, 1), toks].unsqueeze(1).broadcast_to([P, 2, LO, HALF]), ALU.mult)
                last.then_inc(lo_hot, 1)

            def weigh(p, par, gi):
                wait(pool, pt_ok, 4 * p + gi + 1)
                wait(pool, gel_sb, 4 * p + 4)
                g = GG[par][:, :, :, Q32 * gi:Q32 * gi + Q32]
                pool.tensor_tensor(g, g, Pt[gi % 2], ALU.mult).then_inc(g_ok, 1)

            lo_hots(0, 0, 0)
            lo_hots(0, 0, 1)

            def step(p, j, par):
                more = not (isinstance(p, int) and p == T // 2 - 1)
                weigh(p, par, 0)
                weigh(p, par, 1)
                if more:
                    lo_hots(p + 1, 1 - par, 0)
                weigh(p, par, 2)
                weigh(p, par, 3)
                if more:
                    lo_hots(p + 1, 1 - par, 1)

            steps(pool, step, T // 2)

        @block.scalar
        def _(act):
            act.wait_ge(in_w, 16 * 13)
            act.activation(gates[:, 2:4], gates[:, 0:2], ACT.Tanh).then_inc(gates_ok, 1)
            act.wait_ge(std_in, 1)
            act.activation(lnt[:, 2, :], lnt[:, 1, :], ACT.Sqrt).then_inc(std_out, 1)

            def inputs_out(i):
                wait(act, in_T, i + 1)
                wait(act, v_ps, i)
                act.activation(xT, PS[:, 0, 0:P], ACT.Copy)
                src = PS[:, 0, P:2 * P].rearrange("p (b k) -> p b k", b=2)
                act.activation(cT, src.unsqueeze(2).broadcast_to([P, 2, 2, S]), ACT.Copy).then_inc(in_T_sb, 1)

            def q_high(i):
                wait(act, q_ps, i + 1)
                wait(act, row_tile, 4 * i)
                act.activation(Qp.rearrange("p a b -> p (a b)"), PS[:, 1, :], ACT.Copy).then_inc(q_hi, 1)

            def k_high(i):
                wait(act, k_ps, i + 1)
                wait(act, row_tile, 4 * i)
                act.activation(Kp.rearrange("p a b -> p (a b)"), PS[:, 2, :], ACT.Copy).then_inc(k_hi, 1)

            def v_out(i, par):
                wait(act, v_ps, i + 1)
                wait(act, av_ok, i - 1)
                for h2 in range(2):
                    r = slice(64 * h2, 64 * h2 + 64)
                    src = PS[r, 0, 256:512].rearrange("p (b h a d) -> p b h a d", b=2, h=HP, a=2)
                    last = act.activation(Vb[par][r, :, :, h2, 0:HD], src[:, :, :, h2, :], ACT.Copy)
                last.then_inc(v_sb, 1)

            inputs_out(0)
            q_high(0)
            k_high(0)
            act.wait_ge(zeros, 6)
            v_out(0, 0)
            inputs_out(1)
            Ef = E.rearrange("p h k -> p (h k)")
            ETf = ET.rearrange("p h k -> p (h k)")

            def step(i, j, par):
                last = isinstance(i, int) and i == T - 1
                if not last:
                    q_high(i + 1)
                for n in range(2):
                    wait(act, shifted, 2 * i + n + 1)
                    act.activation(Ef[:, 512 * n:512 * n + 512], Ef[:, 512 * n:512 * n + 512], ACT.Exp,
                                   scale=1.0 / SCORE).then_inc(probs, 1)
                    if n == 0 and not last:
                        k_high(i + 1)
                if not last:
                    v_out(i + 1, 1 - par)
                if not (isinstance(i, int) and i < 2):
                    attn_out(i - 2)
                wait(act, av_ok, i)
                for n in range(2):
                    wait(act, e_T, 2 * i + n + 1)
                    act.activation(ETf[:, 512 * n:512 * n + 512], PS[:, 5 + n, :], ACT.Copy).then_inc(e_T_sb, 1)
                if not (isinstance(i, int) and i >= T - 2):
                    inputs_out(i + 2)

            def attn_out(i):
                wait(act, attn_T, i + 1)
                wait(act, wo_ok, i)
                act.activation(aT, PS[:, 1, 0:P], ACT.Copy).then_inc(attn_T_sb, 1)

            steps(act, step, T, lead=4)
            attn_out(T - 2)
            attn_out(T - 1)

            act.wait_ge(std_in, 2)
            act.activation(lnt[:, 2, :], lnt[:, 1, :], ACT.Sqrt).then_inc(std_out, 1)

            def normalise2(c, par):
                wait(act, z_T, c - 1)
                for k in range(2, 4):
                    i = 4 * c + k
                    last = act.activation(zb[par][:, k:k + 1, :], X[:, bass.ds(i, 1), :], ACT.Identity,
                                          bias=lnt[:, 0, bass.ds(i, 1)], scale=rstd[:, bass.ds(i, 1)])
                last.then_inc(z_act, 1)

            act.wait_ge(shift_ok, 1)
            normalise2(0, 0)

            def z_out(c, j, par):
                if not (isinstance(c, int) and c == T // 4 - 1):
                    normalise2(c + 1, 1 - par)
                wait(act, z_T, c + 1)
                act.activation(ZT[:, bass.ds(c * 512, 512)], PS[:, par, :], ACT.Copy).then_inc(z_sb, 1)

            steps(act, z_out, T // 4)
            act.wait_ge(std_in, 3)
            act.activation(bn[:, 7:8], bn[:, 4:5], ACT.Sqrt).then_inc(std_out, 1)
            act.wait_ge(bn_ok, 1)
            act.wait_ge(z_sb, T // 4)

            def picks_out(g):
                wait(act, picks_T, g + 1)
                wait(act, split_ok, g)
                wait(act, rest_ok, g)
                act.activation(codeT.rearrange("p a b -> p (a b)"), PS[:, 2, 0:256], ACT.Copy)
                weights = PS[:, 2, 256:512].rearrange("p (a b) -> p a b", a=2)
                act.activation(w1[:, bass.ds(2 * g, 2), :], weights, ACT.Copy, scale=W_SCALE)
                act.activation(wFull, weights, ACT.Copy, scale=W_SCALE).then_inc(picks_sb, 1)

            def lists_out(g):
                wait(act, split_ok, g + 1)
                act.activation(hi16[:, bass.ds(2 * g, 2), :], codeHL[:, 0], ACT.Copy)
                act.activation(lo16[:, bass.ds(2 * g, 2), :], codeHL[:, 1], ACT.Copy).then_inc(hl_ok, 1)
                wait(act, rest_ok, g + 1)
                act.activation(w2[:, bass.ds(2 * g, 2), :], wRest, ACT.Copy, scale=W2_SCALE).then_inc(w_ok, 1)

            def normed(i, par):
                wait(act, sim_ps, i - 1)
                act.activation(xs[par], ZT[:, bass.ds(i * P, P)], ACT.Identity, bias=bn[:, 6:7],
                               scale=bn[:, 5:6]).then_inc(xs_ok, 1)

            normed(0, 0)

            def exponentials(g):
                wait(act, diff_ok, g + 1)
                act.activation(wgt, wgt, ACT.Exp).then_inc(exp_ok, 1)

            def select(g, first=False, second=False, last=False):
                for k in range(G4):
                    i = G4 * g + k
                    if not (last and k == G4 - 1):
                        normed(i + 1, (k + 1) % 2)
                    wait(act, sim_ps, i + 1)
                    wait(act, idx_ok, i - 1)
                    act.activation(sim[k % 2].rearrange("p a h k -> p (a h k)"), PS[:, k % 2, :], ACT.Copy).then_inc(sim_sb, 1)
                    if not first:
                        if k == 1:
                            exponentials(g - 1)
                            if not second:
                                lists_out(g - 2)
                        if k == 3:
                            picks_out(g - 1)

            select(0, first=True)
            select(1, second=True)
            with act.Fori(2, T // G4 - 1) as g:
                select(g)
            select(T // G4 - 1, last=True)
            exponentials(T // G4 - 1)
            lists_out(T // G4 - 2)
            picks_out(T // G4 - 1)
            lists_out(T // G4 - 1)

            def second_part(p, gi):
                n = 4 * p + gi
                wait(act, p_ps, n + 1)
                wait(act, pt_ok, n - 1)
                act.activation(p2[gi % 2], placed(gi, 1),
                               ACT.Copy, scale=1.0 / W2_SCALE).then_inc(p2_sb, 1)

            def gelu(p, par, k):
                m = 4 * p + k
                wait(act, o_ps, m + 1)
                wait(act, f_ps, p - 1)
                act.activation(GG[par][:, 2 * k:2 * k + 2].rearrange("p l h t -> p (l h t)"), PS[:, 4 + k % 2, :],
                               ACT.Gelu).then_inc(gel_sb, 1)

            for k in range(4):
                gelu(0, 0, k)
            second_part(0, 0)
            second_part(0, 1)

            def step2(p, j, par):
                second_part(p, 2)
                second_part(p, 3)
                if not (isinstance(p, int) and p == T // 2 - 1):
                    for k in range(4):
                        gelu(p + 1, 1 - par, k)
                    second_part(p + 1, 0)
                    second_part(p + 1, 1)

            steps(act, step2, T // 2)

        @block.tensor
        def _(pe):
            pe.wait_ge(ids, 6)
            pe.wait_ge(in_w, 16 * 13)
            for n in range(4):
                last = pe.transpose(PS[:, 0, n * P:n * P + P], wnat[:, n, :], idf)
            last.then_inc(w_T, 1)
            for n in range(4):
                last = pe.transpose(PS[:, 1, n * P:n * P + P], keyn[:, n // 2, n % 2, :], idf)
            last.then_inc(w_T, 1)
            for n in range(LO):
                last = pe.transpose(PS[:, 2 + n // 4, (n % 4) * P:(n % 4) * P + P], kinn[:, n, :], idf)
            last.then_inc(w_T, 1)
            pe.wait_ge(w_T_sb, 2)
            for a in range(2):
                for h in range(FH):
                    c = (a * FH + h) * NK
                    last = pe.matmul(PS[:, 4, c:c + NK], wfn[:, a * FH + h, :],
                                     keyT[:, h // 4, a, (h % 4) * NK:(h % 4) * NK + NK], start=True, stop=True)
            last.then_inc(w2_ps, 1)
            pe.wait_ge(w2_sb, 1)

            pe.wait_ge(const_rows, 32)
            def inputs_T(i, j, par):
                wait(pe, xn_ready, i + 1)
                wait(pe, ctx_in[par], 16 * (j + 1))
                wait(pe, v_sb, i)
                pe.transpose(PS[:, 0, 0:P], xnb[par], idf)
                pe.transpose(PS[:, 0, P:2 * P], cb[par], idf).then_inc(in_T, 1)

            def project(i):
                wait(pe, in_T_sb, i + 1)
                wait(pe, attn_T_sb, i - 3)
                for g in range(HG):
                    last = pe.matmul(PS[:, 1, g * P:g * P + P], WqT[:, g].rearrange("p a b c -> p (a b c)"), xT,
                                     start=True, stop=True)
                last.then_inc(q_ps, 1)
                wait(pe, x2_ok, i - 3)
                for g in range(HG):
                    last = pe.matmul(PS[:, 2, g * P:g * P + P], WkT[:, g].rearrange("p a b c -> p (a b c)"), cT[:, :, 0, :],
                                     start=True, stop=True)
                last.then_inc(k_ps, 1)
                for b in range(2):
                    last = pe.matmul(PS[:, 0, 256 + b * P:256 + b * P + P],
                                     cT[:, b].rearrange("p c k -> p (c k)"), WvT,
                                     start=True, stop=True)
                last.then_inc(v_ps, 1)

            def scores(i, j, par):
                wait(pe, q_sb, i + 1)
                wait(pe, k_sb, i + 1)
                wait(pe, mask_ok, i + 1)
                wait(pe, rows_in[par], 32 * (j + 1))
                wait(pe, shifted, 2 * i)
                for n in range(2):
                    o = PS[:, 3 + n, :]
                    pe.matmul(o, lrow[par], rrow[par][:, 512 * n:512 * n + 512], start=True, stop=False,
                              skip_group_check=True)
                    pe.matmul(o.rearrange("p (h k) -> p h k", k=S), idb, mb[par].unsqueeze(1).broadcast_to([P, 8, S]),
                              start=False, stop=False, skip_group_check=True)
                for k, r4 in enumerate((0, 2, 1, 3)):
                    if k >= 2:
                        pe.wait_ge(row_tile, 4 * i + k - 1)
                    n, r = r4 // 2, slice(32 * r4, 32 * r4 + 32)
                    for g in range(HG):
                        c = (4 * (r4 % 2) + g) * S
                        for b in range(2):
                            last = pe.matmul(PS[64 * b:64 * b + 64, 3 + n, c:c + S],
                                             Qp[r, g, 64 * b:64 * b + 64], Kp[r, g, 64 * b:64 * b + 64],
                                             start=False, stop=(k >= 2 and g == HG - 1), skip_group_check=True)
                    last.then_inc(row_tile, 1)

            def probs_T(i):
                for n in range(2):
                    wait(pe, probs, 2 * i + n + 1)
                    wait(pe, e_T_sb, 2 * i + n - 1)
                    for c in range(4):
                        p = 4 * n + c
                        last = pe.transpose(PS[:, 5 + n, c * P:c * P + P],
                                            E[:, 2 * p:2 * p + 2, :].rearrange("p h k -> p (h k)"), idf)
                    last.then_inc(e_T, 1)

            def values(i, par):
                wait(pe, e_T_sb, 2 * i + 2)
                wait(pe, v_sb, i + 1)
                wait(pe, attn_ok, i)
                for p in range(HP):
                    for b in range(2):
                        last = pe.matmul(PS[64 * b:64 * b + 64, 7, 18 * p:18 * p + 18], ET[:, p, 64 * b:64 * b + 64],
                                         Vb[par][:, b, p].rearrange("p a d -> p (a d)"), start=True, stop=True)
                last.then_inc(av_ok, 1)

            def attn_turn(i):
                wait(pe, attn_ok, i + 1)
                wait(pe, attn_T_sb, i)
                wait(pe, q_sb, min(i + 4, T) if isinstance(i, int) else i + 4)
                pe.transpose(PS[:, 1, 0:P], attn.rearrange("p h d -> p (h d)"), idf).then_inc(attn_T, 1)

            def attn_wo(i):
                wait(pe, attn_T_sb, i + 1)
                wait(pe, x2_ok, i)
                wait(pe, k_sb, min(i + 4, T) if isinstance(i, int) else i + 4)
                pe.matmul(PS[:, 2, 0:P], aT, WoT, start=True, stop=True).then_inc(wo_ok, 1)

            inputs_T(0, 0, 0)
            project(0)
            inputs_T(1, 0, 1)

            def step(i, j, par):
                scores(i, j, par)
                if not (isinstance(i, int) and i == T - 1):
                    project(i + 1)
                if not (isinstance(i, int) and i == 0):
                    values(i - 1, 1 - par)
                if not (isinstance(i, int) and i < 2):
                    attn_turn(i - 2)
                probs_T(i)
                if not (isinstance(i, int) and i < 2):
                    attn_wo(i - 2)
                if not (isinstance(i, int) and i >= T - 2):
                    inputs_T(i + 2, j + 1, par)

            steps(pe, step, T, lead=4)
            values(T - 1, 1)
            attn_turn(T - 2)
            attn_wo(T - 2)
            attn_turn(T - 1)
            attn_wo(T - 1)

            pe.wait_ge(x2_ok, T)

            def z_turn(c, j, par):
                wait(pe, z_ok, c + 1)
                wait(pe, z_act, c + 1)
                wait(pe, z_sb, c - 1)
                for k in range(4):
                    last = pe.transpose(PS[:, par, k * P:k * P + P], zb[par][:, k, :], idf)
                last.then_inc(z_T, 1)

            steps(pe, z_turn, T // 4)

            pe.wait_ge(z_sb, T // 4)
            pe.wait_ge(z_stat, T // 4)

            def picks_turn(g):
                wait(pe, picks_sb, g)
                wait(pe, planes_ok, g + 1)
                for q in range(2):
                    cols = slice(16 * q, 16 * q + 16)
                    for c in range(NC):
                        pe.matmul(PS[:, 2, q * P:q * P + P], planes[:, c, cols, :].rearrange("p a b -> p (a b)"), idh,
                                  start=(c == 0), stop=(c == NC - 1))
                wait(pe, picks_ok, g + 1)
                for q in range(2):
                    cols = slice(16 * q, 16 * q + 16)
                    last = pe.transpose(PS[:, 2, 256 + q * P:256 + q * P + P],
                                        wnorm[:, cols, :].rearrange("p a b -> p (a b)"), idf)
                last.then_inc(picks_T, 1)

            def sims(g, first=False):
                for k in range(G4):
                    i = G4 * g + k
                    wait(pe, xs_ok, i + 1)
                    wait(pe, sim_sb, i - 1)
                    pe.matmul(PS[:, k % 2, :], xs[k % 2], W2, start=True, stop=True).then_inc(sim_ps, 1)
                    if k == 3 and not first:
                        picks_turn(g - 1)

            sims(0, first=True)
            sims(1)
            with pe.Fori(2, T // G4) as g:
                sims(g)
            picks_turn(T // G4 - 1)
            pe.wait_ge(picks_sb, T // G4)

            def expert_in(p, par, k):
                m = 4 * p + k
                wait(pe, gel_sb, m - 1)
                for n in range(2):
                    last = pe.matmul(PS[:, 4 + k % 2, n * 256:n * 256 + 256], kinT[:, 2 * k + n, :],
                                     ZT[:, bass.ds(p * 256, 256)], start=True, stop=True)
                last.then_inc(o_ps, 1)

            def place(p, par, gi):
                q = gi // 2
                n = 4 * p + gi
                wait(pe, a_ok, 2 * p + q + 1)
                wait(pe, lo_hot, 2 * p + q + 1)
                wait(pe, pt_ok, n - 1)
                for t in range(Q32):
                    last = pe.matmul(PS[:, 2 * (gi % 2) + t // 16, 32 * (t % 16):32 * (t % 16) + 32],
                                     A[:, q, :, Q32 * (gi % 2) + t], Bm[par][:, :, :, :, Q32 * gi + t],
                                     start=True, stop=True)
                last.then_inc(p_ps, 1)

            def expert_out(p, par):
                wait(pe, g_ok, 4 * p + 4)
                wait(pe, y_ok, p)
                for half in range(2):
                    for l in range(LO):
                        last = pe.matmul(PS[:, 6, half * P:half * P + P], GG[par][:, l, half, :], kout[:, l, :],
                                         start=(l == 0), stop=(l == LO - 1))
                last.then_inc(f_ps, 1)

            for k in range(4):
                expert_in(0, 0, k)
            place(0, 0, 0)
            place(0, 0, 1)

            def step2(p, j, par):
                place(p, par, 2)
                place(p, par, 3)
                if not (isinstance(p, int) and p == 0):
                    expert_out(p - 1, 1 - par)
                if not (isinstance(p, int) and p == T // 2 - 1):
                    for k in range(4):
                        expert_in(p + 1, 1 - par, k)
                    place(p + 1, 1 - par, 0)
                    place(p + 1, 1 - par, 1)

            steps(pe, step2, T // 2)
            expert_out(T // 2 - 1, 1)

        @block.vector
        def _(dve):
            ch = Chain(dve, dve0)

            def layernorm_scale(which, done):
                me, m2e, mo, m2o = (stats[:, :, n] for n in (1, 2, 4, 5))
                ch.add(dve.tensor_tensor(mean, me, mo, ALU.add))
                ch.add(dve.tensor_tensor(lnt[:, 0, :], me, mo, ALU.subtract))
                ch.add(dve.tensor_tensor(lnt[:, 1, :], m2e, m2o, ALU.add))
                ch.settle()
                ch.add(dve.tensor_scalar(mean, mean, 0.5, None, ALU.mult))
                ch.add(dve.tensor_tensor(lnt[:, 0, :], lnt[:, 0, :], lnt[:, 0, :], ALU.mult))
                ch.add(dve.tensor_scalar(lnt[:, 1, :], lnt[:, 1, :], 1.0 / D, EPS, ALU.mult, ALU.add))
                ch.settle()
                dve.scalar_tensor_tensor(lnt[:, 1, :], lnt[:, 0, :], 0.25, lnt[:, 1, :], ALU.mult, ALU.add).then_inc(std_in, 1)
                dve.wait_ge(std_out, done)
                ch.link(dve.reciprocal(rstd, lnt[:, 2, :]))

            dve.wait_ge(in_p, 80)
            ch.link(dve.tensor_copy(posF, posI))
            for h in range(H):
                ch.add(dve.tensor_scalar(kbias[:, h, :], posF[:, 1, :], SLOPES[h] * SCORE, None, ALU.mult))
            for par in range(2):
                ch.add(dve.tensor_copy(rrow[par][0:QROWS, :], srow_f))
            ch.add(dve.tensor_copy(brow_b, brow_f))
            ch.settle()
            kf = kbias.rearrange("p h k -> p (h k)")
            for n in range(3):
                ch.add(dve.tensor_copy(kparts[:, n, :], kf))
                ch.add(dve.tensor_copy(qparts[:, n, :], posF[:, 0, :]))
                ch.settle()
                if n < 2:
                    ch.add(dve.tensor_tensor(kf, kf, kparts[:, n, :], ALU.subtract))
                    ch.add(dve.tensor_tensor(posF[:, 0, :], posF[:, 0, :], qparts[:, n, :], ALU.subtract))
                    ch.settle()
            dve.sem_inc(parts_ok, 1)
            dve.wait_ge(zeros, 6)
            dve.wait_ge(w_T, 1)
            for n, (w, scale) in enumerate(((WqT, QK_SCALE / float(np.sqrt(HD))), (WkT, QK_SCALE))):
                for copy in range(4):
                    dve.tensor_scalar(w[:, :, :, copy, :], PS[:, 0, n * P:n * P + P].rearrange("p (r g d) -> p g r d", g=HG, r=4),
                                      scale, None, ALU.mult)
            dve.tensor_copy(WvT, PS[:, 0, 2 * P:3 * P])
            dve.tensor_copy(WoT, PS[:, 0, 3 * P:4 * P]).then_inc(w_T_sb, 1)
            dve.wait_ge(w_T, 2)
            dve.tensor_copy(keyT.rearrange("p a b k -> p (a b k)"), PS[:, 1, :]).then_inc(w_T_sb, 1)
            dve.wait_ge(w_T, 3)
            dve.tensor_copy(kinT.rearrange("p a b -> p (a b)"), PS[:, 2:4, :].rearrange("p a b -> p (a b)")).then_inc(w_T_sb, 1)
            dve.wait_ge(gates_ok, 1)
            ch.add(dve.tensor_scalar(gates[:, 3:4], gates[:, 3:4], 1.0 / W_SCALE, None, ALU.mult))
            for i in range(T):
                if i % XPIECE == 0:
                    dve.wait_ge(in_x[i // XPIECE], 16)
                dve.bn_stats(stats[:, i:i + 1, :], X[:, i:i + 1, :]).then_inc(stat_ok, 1)
            dve.wait_ge(w2_ps, 1)
            dve.tensor_copy(W2, PS[:, 4, :]).then_inc(w2_sb, 1)
            dve.wait_ge(stat_ok, T)
            layernorm_scale(0, 1)

            dve.wait_ge(in_m[0], 16)

            def normalise(i, par):
                wait(dve, in_T, i - 1)
                dve.tensor_scalar(xnb[par].unsqueeze(1), X[:, bass.ds(i, 1), :], mean[:, bass.ds(i, 1)], rstd[:, bass.ds(i, 1)],
                                  ALU.subtract, ALU.mult).then_inc(xn_ready, 1)

            def mask_term(i, par):
                wait(dve, row_tile, 4 * i - 4)
                dve.tensor_scalar(mb[par].unsqueeze(1), maskI[:, bass.ds(i, 1), :], 0.0, MASKED, ALU.is_equal,
                                  ALU.mult).then_inc(mask_ok, 1)

            def q_low(i):
                wait(dve, q_hi, i + 1)
                dve.scalar_tensor_tensor(Qp.rearrange("p a b -> p (a b)"), Qp.rearrange("p a b -> p (a b)"), low[:, 0:1],
                                         PS[:, 1, :], ALU.mult, ALU.add).then_inc(q_sb, 1)

            def k_low(i):
                wait(dve, k_hi, i + 1)
                dve.scalar_tensor_tensor(Kp.rearrange("p a b -> p (a b)"), Kp.rearrange("p a b -> p (a b)"), low[:, 1:2],
                                         PS[:, 2, :], ALU.mult, ALU.add).then_inc(k_sb, 1)

            def residual(i):
                wait(dve, wo_ok, i + 1)
                xi = X[:, bass.ds(i, 1), :]
                dve.scalar_tensor_tensor(xi, PS[:, 2, 0:P].unsqueeze(1), gates[:, 2:3], xi, ALU.mult,
                                         ALU.add).then_inc(x2_ok, 1)
                wait(dve, x2_ok, i + 1)
                dve.bn_stats(stats[:, bass.ds(i, 1), :], xi).then_inc(stat_ok, 1)

            normalise(0, 0)
            normalise(1, 1)
            mask_term(0, 0)
            q_low(0)
            k_low(0)
            LINKS = 3
            link1 = Chain(dve, dve1)

            def step(i, j, par):
                link1.at(0 if isinstance(i, int) and i == 0 else LINKS * i - 2)
                if isinstance(i, int) and i == 3:
                    dve.wait_ge(in_m[1], 16)
                wait(dve, row_tile, 4 * i + 4)
                s = PS[:, 3:5, :].rearrange("p b (h k) -> p (b h) k", k=S)
                link1.add(dve.tensor_reduce(smax, s, AX.X, ALU.max))
                if not (isinstance(i, int) and i == T - 1):
                    mask_term(i + 1, 1 - par)
                link1.settle()
                wait(dve, e_T, 2 * i)
                for n in range(2):
                    hs = slice(8 * n, 8 * n + 8)
                    dve.tensor_tensor(E[:, hs, :], s[:, hs, :], rows(smax[:, hs], S), ALU.subtract).then_inc(shifted, 1)
                if not (isinstance(i, int) and i == T - 1):
                    q_low(i + 1)
                    k_low(i + 1)
                if not (isinstance(i, int) and i >= T - 2):
                    normalise(i + 2, par)
                if not (isinstance(i, int) and i == 0):
                    attended(i - 1)
                    assert link1.n == LINKS
                if not (isinstance(i, int) and i < 2):
                    residual(i - 2)

            def attended(i):
                wait(dve, av_ok, i + 1)
                o = PS[:, 7, 0:144].rearrange("p (h e) -> p h e", e=HD + 1)
                link1.link(dve.tensor_scalar(den, o[:, :, HD], 1.0, None, ALU.add))
                link1.link(dve.reciprocal(den, den))
                wait(dve, attn_T, i)
                dve.tensor_tensor(attn, o[:, :, 0:HD], rows(den, HD), ALU.mult).then_inc(attn_ok, 1)

            steps(dve, step, T, lead=4)
            link1.at(LINKS * T - 2)
            attended(T - 1)
            residual(T - 2)
            residual(T - 1)

            dve.wait_ge(stat_ok, 2 * T)
            layernorm_scale(1, 2)
            dve.scalar_tensor_tensor(lnt[:, 0, :], mean, -1.0, rstd, ALU.mult, ALU.mult).then_inc(shift_ok, 1)

            def normalise2(c, par):
                wait(dve, z_T, c - 1)
                for k in range(2):
                    i = 4 * c + k
                    last = dve.tensor_scalar(zb[par][:, k:k + 1, :], X[:, bass.ds(i, 1), :], mean[:, bass.ds(i, 1)],
                                             rstd[:, bass.ds(i, 1)], ALU.subtract, ALU.mult)
                last.then_inc(z_ok, 1)

            normalise2(0, 0)

            def step1b(c, j, par):
                if not (isinstance(c, int) and c == T // 4 - 1):
                    normalise2(c + 1, 1 - par)
                wait(dve, z_sb, c + 1)
                dve.bn_stats(stats[:, bass.ds(c, 1), :], ZT[:, bass.ds(c * 512, 512)]).then_inc(z_stat, 1)

            steps(dve, step1b, T // 4)
            dve.wait_ge(z_stat, T // 4)
            ch.link(dve.bn_aggr(bn[:, 2:4], stats[:, 0:T // 4, :].rearrange("p a b -> p (a b)")))
            dve.tensor_scalar(bn[:, 4:5], bn[:, 3:4], EPS, None, ALU.add).then_inc(std_in, 1)
            dve.wait_ge(std_out, 3)
            ch.link(dve.reciprocal(bn[:, 4:5], bn[:, 7:8]))
            ch.link(dve.tensor_tensor(bn[:, 5:6], bn[:, 4:5], bn[:, 0:1], ALU.mult))
            ch.link(dve.tensor_tensor(bn[:, 7:8], bn[:, 5:6], bn[:, 2:3], ALU.mult))
            dve.tensor_tensor(bn[:, 6:7], bn[:, 1:2], bn[:, 7:8], ALU.subtract).then_inc(bn_ok, 1)

            dve.wait_ge(iota_ok, 3)
            link2 = Chain(dve, dve2)

            def split(g):
                wait(dve, picks_sb, g + 1)
                wait(dve, hl_ok, g)
                dve.tensor_scalar(codeHL[:, 0], codeT, 3, None, ALU.logical_shift_right)
                dve.tensor_scalar(codeHL[:, 1], codeT, LO - 1, None, ALU.bitwise_and).then_inc(split_ok, 1)

            def pick(k):
                for h in range(FH):
                    last = dve.max_index(pk[:, k * FH + h, :], val[:, k * FH + h, :], cand[k % 2][:, h])
                link2.add(last)

            def decode(g):
                wait(dve, picks_T, g)
                link2.settle()
                for c, (a, b) in enumerate(PAIRS):
                    k0 = (a + 1) * (b + 1) - 1
                    last = dve.tensor_scalar(planes[:, c, :, k0:K8], pk[:, :, k0:K8], float(c), None, ALU.is_equal)
                last.then_inc(picks_hot, 1)
                wait(dve, exp_ok, g + 1)
                wait(dve, picks_ok, g)
                link2.add(dve.tensor_reduce(wsum, wgt, AX.X, ALU.add))

            def select(g, first=False):
                for k in range(G4):
                    i = G4 * g + k
                    par = k % 2
                    wait(dve, sim_sb, i + 1)
                    dve.nop(nofuse=True)
                    for a in range(2):
                        for h in range(FH):
                            last = dve.max(s8[par][:, a, h, :], sim[par][:, a, h, :])
                    link2.add(last)
                    if not (first and k == 0):
                        link2.settle(but=1)
                        dve.nop(nofuse=True)
                        pick((k - 1) % G4)
                        link2.settle(but=1)
                    else:
                        link2.settle()
                    for at, ra, rb in BLOCKS:
                        na, nb = ra.stop - ra.start, rb.stop - rb.start
                        last = dve.tensor_tensor(cand[par][:, :, at:at + na * nb].rearrange("p h (a b) -> p h a b", a=na),
                                                 rows(s8[par][:, 0, :, ra], nb),
                                                 s8[par][:, 1, :, rb].unsqueeze(2).broadcast_to([P, FH, na, nb]), ALU.add)
                    link2.add(last)
                    if k == 0:
                        wait(dve, ccode_ok, g)
                        dve.nop(nofuse=True)
                    for a in range(2):
                        for h in range(FH):
                            last = dve.max_index(i8[:, a, k * FH + h, :], s8[par][:, a, h, :], sim[par][:, a, h, :])
                    last.then_inc(idx_ok, 1)
                    if k == 0 and not first:
                        decode(g - 1)
                    link2.settle()
                    if k == 0:
                        wait(dve, diff_ok, g)
                    dve.nop(nofuse=True)
                    for h in range(FH):
                        last = dve.max(val[:, k * FH + h, :], cand[par][:, h])
                    link2.add(last)
                    if k == G4 - 1:
                        link2.settle()
                        dve.sem_inc(val_ok, 1)
                    if k == 0 and not first:
                        dve.reciprocal(wsum, wsum).then_inc(rsum_ok, 1)
                    if k == 3 and not first:
                        split(g - 1)

            EACH = 4 * G4 + 1
            link2.at(0)
            select(0, first=True)
            assert link2.n == EACH - 2, link2.n
            link2.at(EACH - 2)
            select(1)
            with dve.Fori(2, T // G4) as g:
                link2.at(g * EACH - 2)
                select(g)
                assert link2.n == EACH, link2.n
            link2.at(EACH * (T // G4) - 2)
            link2.settle()
            pick(G4 - 1)
            decode(T // G4 - 1)
            link2.settle()
            dve.reciprocal(wsum, wsum).then_inc(rsum_ok, 1)
            split(T // G4 - 1)
            dve.wait_ge(hl_ok, T // G4)
            dve.wait_ge(oh_zero, 1)

            def hi_hots(p, q):
                wait(dve, p_ps, 4 * p + 2 * q - 2)
                src = hi16[:, bass.ds(p, 1), HALF * q:HALF * q + HALF]
                for n in range(2):
                    v = slice(64 * n, 64 * n + 64)
                    last = dve.tensor_tensor(A[:, q, v, :], src.broadcast_to([P, 64, HALF]), iota[:, v, :], ALU.is_equal)
                last.then_inc(a_ok, 1)

            def joined(p, gi):
                n = 4 * p + gi
                wait(dve, p2_sb, n + 1)
                wait(dve, g_ok, n - 1)
                dve.tensor_tensor(Pt[gi % 2], placed(gi, 0), p2[gi % 2], ALU.add).then_inc(pt_ok, 1)

            def finish(p, j, par):
                wait(dve, f_ps, p + 1)
                wait(dve, y_out[par], 16 * j)
                dve.scalar_tensor_tensor(yb[par], PS[:, 6, 0:256].rearrange("p (a d) -> p a d", a=2), gates[:, 3:4],
                                         X[:, bass.ds(2 * p, 2), :], ALU.mult, ALU.add).then_inc(y_ok, 1)

            def lo_ones(p):
                wait(dve, lo_hot, 2 * p)
                for half in range(2):
                    r = slice(64 * half, 64 * half + 64)
                    last = dve.tensor_tensor(oh[r, half], lo16[r, bass.ds(p, 1), :].broadcast_to([64, LO, P]), iotaL[r],
                                             ALU.is_equal)
                last.then_inc(oh_ok, 1)

            lo_ones(0)
            hi_hots(0, 0)
            hi_hots(0, 1)

            def step2(p, j, par):
                more = not (isinstance(p, int) and p == T // 2 - 1)
                joined(p, 0)
                joined(p, 1)
                if more:
                    lo_ones(p + 1)
                    hi_hots(p + 1, 0)
                joined(p, 2)
                joined(p, 3)
                if not (isinstance(p, int) and p == 0):
                    finish(p - 1, j if par else j - 1, 1 - par)
                if more:
                    hi_hots(p + 1, 1)

            steps(dve, step2, T // 2, lead=4)
            finish(T // 2 - 1, T // 4 - 1, 1)


_INS = ["x", "ctx_1024", "itok_BxS_8_8191", "itok_BxS2_1_8191", "mask_BxSxS2_if1", "g_xattn", "g_ffn", "L0_xattn_W_q",
        "L0_xattn_W_k", "L0_xattn_W_v", "L0_xattn_W_o", "L0_ffn_gamma", "L0_ffn_beta", "L0_ffn_w_q", "L0_ffn_keys",
        "L0_ffn_key_in", "L0_ffn_key_out"]


def kernel(**inputs):
    import concourse.bacc as bacc
    from concourse.bass_utils import run_bass_kernel_spmd

    nc = bacc.Bacc("TRN2", target_bir_lowering=False, num_devices=1)
    arrays, args = {}, []
    given = [(n, inputs[n]) for n in _INS] + list(zip(("slope_rows", "of_batch", "low_rows"), shape_constants()))
    for name, a in given:
        a = np.ascontiguousarray(a)
        arrays[f"in_{name}"] = a
        args.append(nc.dram_tensor(f"in_{name}", a.shape, mybir.dt.from_np(a.dtype), kind="ExternalInput").ap())
    args.append(nc.dram_tensor("out_0", (B, S, D), F32, kind="ExternalOutput").ap())
    gated_block(nc, *args)
    r = run_bass_kernel_spmd(nc, [arrays], core_ids=[0])
    return r.results[0]["out_0"]
```

```python
import concourse.bass as bass
from concourse import mybir
from contextlib import ExitStack
import numpy as np

F32 = mybir.dt.float32
BF16 = mybir.dt.bfloat16
F16 = mybir.dt.float16
I32 = mybir.dt.int32
U16 = mybir.dt.uint16
ALU = mybir.AluOpType
ACT = mybir.ActivationFunctionType
AX = mybir.AxisListType

P = 128
B, S, D = 128, 64, 128
T = B * S // P
H, HD = 16, 8
HG = H // 4
HP = H // 2
XPIECE = 8
FH, NK, K8 = 8, 32, 8
LO = NK * NK // P
QROWS, KROWS = 9, 6
ROWS = QROWS + KROWS
G4 = 4
NG = T // G4
PAIRS = [(a, b) for a in range(K8) for b in range(K8) if (a + 1) * (b + 1) <= K8]
NC = len(PAIRS)
BLOCKS = [(0, slice(0, 1), slice(0, 8)), (8, slice(1, 2), slice(0, 4)), (12, slice(2, 4), slice(0, 2)),
          (16, slice(4, 8), slice(0, 1))]
HALF = P // 2
Q32 = P // 4
MASKED = -1.0e30
EPS = 1e-5
W_SCALE = 2.0 ** 14
W2_SCALE = 2.0 ** 11
QK_SCALE = 2.0 ** 4
SCORE = QK_SCALE ** 2
SLOPES = [float(np.float32((2.0 ** (-8.0 / H)) ** i)) for i in range(1, H + 1)]


def bf16_parts(v):
    out, rest = [], np.asarray(v, np.float32)
    for _ in range(3):
        top = (rest.view(np.uint32) & np.uint32(0xFFFF0000)).view(np.float32)
        out.append(top)
        rest = rest - top
    return out


def shape_constants():
    s = bf16_parts(-np.asarray(SLOPES, np.float32) * np.float32(SCORE))
    slope_rows = np.stack([np.repeat(s[j], S) for _ in range(3) for j in range(3)])
    of_batch = np.zeros((KROWS, P), np.float32)
    of_batch[0:3, 0:S] = 1.0
    of_batch[3:6, S:P] = 1.0
    return np.ascontiguousarray(slope_rows, np.float32), of_batch


def wait(eng, sem, value):
    if not (isinstance(value, int) and value <= 0):
        eng.wait_ge(sem, value)


def steps(eng, body, n, lead=2, tail=2):
    for i in range(lead):
        body(i, i // 2, i % 2)
    with eng.Fori(lead // 2, (n - tail) // 2) as j:
        for par in range(2):
            body(2 * j + par, j, par)
    for i in range(n - tail, n):
        body(i, i // 2, i % 2)


def group_steps(eng, body):
    for i in range(2 * G4):
        body(i, 0, i)
    with eng.Fori(1, NG // 2 - 1) as j:
        for u in range(2 * G4):
            body(2 * G4 * j + u, j, u)
    for u in range(2 * G4):
        body(T - 2 * G4 + u, NG // 2 - 1, u)


def known(i):
    return isinstance(i, int)


class Chain:

    def __init__(self, eng, sem, start=0):
        self.eng, self.sem, self.base, self.n = eng, sem, start, 0

    def at(self, base):
        self.base, self.n = base, 0

    def add(self, ins):
        self.n += 1
        ins.then_inc(self.sem, 1)

    def settle(self, but=0):
        wait(self.eng, self.sem, self.base + self.n - but)

    def link(self, ins):
        self.add(ins)
        self.settle()


def rows(ap, count):
    s = list(ap.shape)
    return ap.unsqueeze(len(s)).broadcast_to(s + [count])


def gated_block(nc, x, ctx, qpos, kpos, mask, g_x, g_f, wq, wk, wv, wo, gamma, beta, w_ffn, keys,
                key_in, key_out, slope_rows, of_batch, out):
    x_t = x.rearrange("(i c) s d -> (c s) i d", c=2)
    ctx_t = ctx.rearrange("(i c) s d -> (c s) i d", c=2)
    mask_t = mask.rearrange("(i c) q k -> (c q) i k", c=2)
    out_t = out.rearrange("(i c) s d -> (c s) i d", c=2)
    krows_d = nc.dram_tensor("krows_d", (B, 3, H * S), BF16, kind="Internal").ap()
    qrows_d = nc.dram_tensor("qrows_d", (B, 3, 3, S), BF16, kind="Internal").ap()
    q_d = nc.dram_tensor("q_d", (2, P, 2, G4 * P), F16, kind="Internal").ap()
    k_d = nc.dram_tensor("k_d", (2, P, 2, G4 * P), F16, kind="Internal").ap()
    krows_t = krows_d.rearrange("(i c) p n -> i (c p) n", c=2)
    qrows_t = qrows_d.rearrange("(i c) a b q -> i (a b) c q", c=2)

    es = ExitStack()
    with es:
        def sb(name, shape, dt=F32):
            return es.enter_context(nc.sbuf_tensor(name, shape, dt))[:]

        def sem(name):
            return es.enter_context(nc.semaphore(name))

        X = sb("X", [P, T, D])
        ZT = sb("ZT", [P, T * P])
        idf = sb("idf", [P, P])
        idb = sb("idb", [P, P], BF16)
        idh = sb("idh", [P, P], F16)
        stats = sb("stats", [P, T, 6])
        lnt = sb("lnt", [P, 3, T])
        mean = sb("mean", [P, T])
        rstd = sb("rstd", [P, T])
        W2 = sb("W2", [P, 2 * FH * NK])
        kinT = sb("kinT", [P, LO, P])
        kout = sb("kout", [P, LO, D])
        gates = sb("gates", [P, 4])
        bn = sb("bn", [P, 8])
        A = sb("A", [P, 2, P, HALF], F16)
        WORDS = 24576
        AR = sb("AR", [P, WORDS])

        def carver(area, total, start=0):
            at = [start]

            def carve(shape, dt=F32):
                n = int(np.prod(shape[1:]))
                words = n if dt in (F32, I32) else (n + 1) // 2
                v = area[0:shape[0], at[0]:at[0] + words]
                at[0] += (words + 7) // 8 * 8
                assert at[0] <= total, at[0]
                if dt != F32:
                    v = v.bitcast(dt)
                if len(shape) > 2:
                    names = "abcd"[:len(shape) - 1]
                    v = v.rearrange(f"p ({' '.join(names)}) -> p {' '.join(names)}",
                                    **{c: shape[1 + q] for q, c in enumerate(names)})
                return v
            return carve, at

        carve, _ = carver(AR, WORDS)
        WqT = carve([P, HG, 4, HD])
        WkT = carve([P, HG, 4, HD])
        WvT = carve([P, D])
        WoT = carve([P, D])
        maskI = carve([P, T, S], I32)
        cb = [carve([P, G4, D]) for _ in range(2)]
        xnb = carve([P, G4, D])
        lrow = [carve([ROWS, P], BF16) for _ in range(2)]
        rrow = [carve([ROWS, H * S], BF16) for _ in range(2)]
        mb = [carve([P, S], BF16) for _ in range(2)]
        xT = carve([P, G4 * P])
        cT = carve([P, G4, 2, 2, S])
        QHL = carve([P, 2, G4 * P], F16)
        KHL = carve([P, 2, G4 * P], F16)
        Qp = [carve([P, HG, G4 * P], F16) for _ in range(2)]
        Kp = [carve([P, HG, G4 * P], F16) for _ in range(2)]
        Vall = carve([P, 2 * G4 * 2 * HP, 2, HD + 1])
        Vt = Vall.rearrange("p (g t b h) a d -> p g t b h (a d)", g=2, t=G4, b=2)
        E = carve([P, H, S])
        ET = carve([P, HP, P])
        smax = carve([P, H])
        den = carve([P, H])
        attn = carve([P, H, HD])
        aT = carve([P, P])
        zcarve, _ = carver(ZT, T * P)
        wnat = zcarve([P, 4, D])
        wfn = A.rearrange("p a v t -> p (a v t)").bitcast(F32)[:, 0:2 * FH * D].rearrange("p (m d) -> p m d", d=D)
        keyn = zcarve([P, 2, 2, D])
        keyT = zcarve([P, 2, 2, P])
        kinn = zcarve([P, LO, D])
        posI = zcarve([P, 2, S], I32)
        posF = zcarve([P, 2, S])
        kbias = zcarve([P, H, S])
        kparts = zcarve([P, 3, H * S], BF16)
        qparts = zcarve([P, 3, S], BF16)
        srow_f = zcarve([QROWS, H * S])
        brow_f = zcarve([KROWS, P])
        brow_b = zcarve([KROWS, P], BF16)
        carve, at = carver(AR, WORDS)
        iota = carve([P, P, HALF], F16)
        iotaL = carve([P, LO, P], F16)
        hi16 = carve([P, T // 2, P], F16)
        lo16 = carve([P, T // 2, P], F16)
        w1 = carve([P, T // 2, P], F16)
        w2 = carve([P, T // 2, P], F16)
        shared = at[0]
        zb = [carve([P, 4, D]) for _ in range(2)]
        xs = [carve([P, P]) for _ in range(2)]
        sim = [carve([P, 2, FH, NK]) for _ in range(2)]
        s8 = [carve([P, 2, FH, K8]) for _ in range(2)]
        i8 = carve([P, 2, G4 * FH, K8], U16)
        i8f = carve([P, 2, G4 * FH, K8], F16)
        cand = [carve([P, FH, NC]) for _ in range(2)]
        ccode = carve([P, G4 * FH, NC], F16)
        val = carve([P, G4 * FH, K8])
        pk = carve([P, G4 * FH, K8], U16)
        planes = carve([P, NC, G4 * FH, K8], F16)
        wgt = carve([P, G4 * FH, K8])
        wnorm = carve([P, G4 * FH, K8])
        wsum = carve([P, G4 * FH])
        codeT = carve([P, 2, P], U16)
        codeHL = carve([P, 2, 2, P], U16)
        wRest = carve([P, 2, P])
        wFull = carve([P, 2, P])
        carve, at = carver(AR, WORDS, shared)
        Bm = [carve([P, 2, 2, LO, P], F16) for _ in range(2)]
        oh = carve([P, 2, LO, P], F16)
        GG = [carve([P, LO, 2, P]) for _ in range(2)]
        p2 = [carve([P, LO, 2, Q32]) for _ in range(2)]
        Pt = [carve([P, LO, 2, Q32]) for _ in range(2)]
        yb = [carve([P, 2, D]) for _ in range(2)]

        PS = es.enter_context(nc.psum_tensor("PS", [P, 8, 512], F32))[:]

        in_w, in_p = sem("in_w"), sem("in_p")
        in_m = [sem(f"in_m{n}") for n in range(2)]
        in_x = [sem(f"in_x{n}") for n in range(T // XPIECE)]
        ids, zeros, const_rows, prep = sem("ids"), sem("zeros"), sem("const_rows"), sem("prep")
        w_T, w_T_sb, f_T, f_T_sb, gates_ok = (sem(n) for n in ("w_T", "w_T_sb", "f_T", "f_T_sb", "gates_ok"))
        parts_ok, parts_out, std_in, std_out = (sem(n) for n in ("parts_ok", "parts_out", "std_in", "std_out"))
        ctx_in = [sem(f"ctx_in{n}") for n in range(2)]
        rows_in = [sem(f"rows_in{n}") for n in range(2)]
        xn_ready, x_T, c_T, x_T_sb, c_T_sb = (sem(n) for n in ("xn_ready", "x_T", "c_T", "x_T_sb", "c_T_sb"))
        q_wr, k_wr, qk_in = sem("q_wr"), sem("k_wr"), sem("qk_in")
        q_ps, k_ps, v_ps, q_hi, k_hi, q_sb, k_sb, v_sb = (
            sem(n) for n in ("q_ps", "k_ps", "v_ps", "q_hi", "k_hi", "q_sb", "k_sb", "v_sb"))
        mask_ok, shifted, probs = (sem(n) for n in ("mask_ok", "shifted", "probs"))
        e_T, e_T_sb, av_ok, attn_ok = (sem(n) for n in ("e_T", "e_T_sb", "av_ok", "attn_ok"))
        attn_T, attn_T_sb, wo_ok, x2_ok, stat_ok = (
            sem(n) for n in ("attn_T", "attn_T_sb", "wo_ok", "x2_ok", "stat_ok"))
        dve0, dve1, dve2 = (sem(f"dve{n}") for n in range(3))
        z_ok, z_T, z_sb, z_stat, bn_ok = (sem(n) for n in ("z_ok", "z_T", "z_sb", "z_stat", "bn_ok"))
        xs_ok, sim_ps, sim_sb = (sem(n) for n in ("xs_ok", "sim_ps", "sim_sb"))
        idx_ok, val_ok, ccode_ok, planes_ok, diff_ok, exp_ok, rsum_ok = (
            sem(n) for n in ("idx_ok", "val_ok", "ccode_ok", "planes_ok", "diff_ok", "exp_ok", "rsum_ok"))
        picks_ok, picks_T, picks_sb, split_ok, hl_ok, w_ok, rest_ok, oh_zero = (
            sem(n) for n in ("picks_ok", "picks_T", "picks_sb", "split_ok", "hl_ok", "w_ok", "rest_ok", "oh_zero"))
        s8_ok, cand_ok, iota_ok = sem("s8_ok"), sem("cand_ok"), sem("iota_ok")
        picks_hot = sem("picks_hot")
        planes_last = sem("planes_last")
        z_act, shift_ok = sem("z_act"), sem("shift_ok")
        a_ok, p_ps, p2_sb, pt_ok, g_ok = (sem(n) for n in ("a_ok", "p_ps", "p2_sb", "pt_ok", "g_ok"))
        o_ps, gel_sb, f_ps, y_ok = (sem(n) for n in ("o_ps", "gel_sb", "f_ps", "y_ok"))
        row_tile, poolc = sem("row_tile"), sem("poolc")
        oh_ok, lo_hot, lo_first = sem("oh_ok"), sem("lo_hot"), sem("lo_first")
        y_out = [sem(f"y_out{n}") for n in range(2)]

        def placed(gi, part):
            two = PS[:, 2 * (gi % 2):2 * (gi % 2) + 2, :].rearrange("p b n -> p (b n)")
            return two.rearrange("p (t a c l) -> p l a c t", a=2, c=2, l=LO)[:, :, :, part, :]

        block = es.enter_context(nc.Block())

        @block.sync
        def _(sp):
            sp.dma_start(posI[:, 0, :], qpos).then_inc(in_p, 16)
            sp.dma_start(posI[:, 1, :], kpos).then_inc(in_p, 16)
            sp.dma_start(srow_f, slope_rows).then_inc(in_p, 16)
            sp.dma_start(brow_f, of_batch).then_inc(in_p, 16)
            for n, w in enumerate((wq, wk, wv, wo)):
                sp.dma_start(wnat[:, n, :], w).then_inc(in_w, 16)
            sp.dma_start(gates[:, 0:1], g_x.unsqueeze(0).broadcast_to([P, 1])).then_inc(in_w, 16)
            sp.dma_start(gates[:, 1:2], g_f.unsqueeze(0).broadcast_to([P, 1])).then_inc(in_w, 16)
            sp.dma_start(bn[:, 0:1], gamma.unsqueeze(1)).then_inc(in_w, 16)
            sp.dma_start(bn[:, 1:2], beta.unsqueeze(1)).then_inc(in_w, 16)
            sp.dma_start(wfn, w_ffn.rearrange("(m p) d -> p m d", p=P)).then_inc(in_w, 16)
            for a in range(2):
                sp.dma_start(keyn[:, a, :, :], keys[4 * a:4 * a + 4].rearrange("h k a d -> (h k) a d")).then_inc(in_w, 16)
            sp.dma_start(kinn, key_in.rearrange("(p l) d -> p l d", l=LO)).then_inc(in_w, 16)
            sp.dma_start(kout, key_out.rearrange("(p l) d -> p l d", l=LO)).then_inc(in_w, 16)
            def load_ctx(n, par):
                wait(sp, c_T, n - 1)
                sp.dma_start(cb[par], ctx_t[:, bass.ds(G4 * n, G4), :]).then_inc(ctx_in[par], 16)

            def load_x(n):
                sp.dma_start(X[:, n:n + XPIECE, :], x_t[:, n:n + XPIECE, :]).then_inc(in_x[n // XPIECE], 16)

            load_x(0)
            load_ctx(0, 0)
            sp.dma_start(maskI[:, 0:XPIECE, :], mask_t[:, 0:XPIECE, :]).then_inc(in_m[0], 16)
            load_x(XPIECE)
            load_ctx(1, 1)
            sp.wait_ge(parts_ok, 1)
            sp.dma_start(krows_d, kparts).then_inc(parts_out, 16)
            for b in range(3):
                sp.dma_start(qrows_d[:, :, b, :], qparts).then_inc(parts_out, 16)
            for par in range(2):
                sp.dma_start(lrow[par][QROWS:ROWS, :], brow_b).then_inc(const_rows, 16)
            for n in range(2 * XPIECE, T, XPIECE):
                load_x(n)
            sp.wait_ge(parts_out, 64)

            def load_rows(i, par):
                wait(sp, row_tile, 4 * i - 4)
                sp.dma_start(rrow[par][QROWS:ROWS, :], krows_t[i, :, :]).then_inc(rows_in[par], 16)
                sp.dma_start(lrow[par][0:QROWS, :].rearrange("r (c q) -> r c q", c=2), qrows_t[i, :, :, :]).then_inc(rows_in[par], 16)

            def parts_to_dram(n, par):
                wait(sp, q_sb, n + 1)
                sp.nop(nofuse=True)
                wait(sp, qk_in, 128 * n)
                sp.dma_start(q_d[par], QHL).then_inc(q_wr, 16)
                wait(sp, k_sb, n + 1)
                sp.dma_start(k_d[par], KHL).then_inc(k_wr, 16)

            def copies_back(n, par):
                wait(sp, row_tile, 16 * (n - 1))
                sp.nop(nofuse=True)
                for sem_wr, src, dst, part in ((q_wr, q_d, Qp, (0, 0, 1, 1)), (k_wr, k_d, Kp, (0, 1, 0, 1))):
                    wait(sp, sem_wr, 16 * (n + 1))
                    for c in range(4):
                        sp.dma_start(dst[par][c:P:4], src[par].rearrange("(g p) a t -> a p g t", g=HG)[part[c]]).then_inc(qk_in, 16)

            load_rows(0, 0)
            load_rows(1, 1)
            parts_to_dram(0, 0)
            copies_back(0, 0)
            sp.dma_start(maskI[:, XPIECE:, :], mask_t[:, XPIECE:, :]).then_inc(in_m[1], 16)

            def load(i, j, u):
                q, s = 2 * j + u // G4, u % G4
                if not (known(i) and i + 2 >= T):
                    load_rows(i + 2, u % 2)
                if s == 0 and not (known(q) and q + 2 >= NG):
                    load_ctx(q + 2, u // G4)
                if s == 0 and not (known(q) and q + 1 >= NG):
                    parts_to_dram(q + 1, 1 - u // G4)
                if s == 1 and not (known(q) and q + 1 >= NG):
                    copies_back(q + 1, 1 - u // G4)

            group_steps(sp, load)

            def store(p, j, par):
                wait(sp, y_ok, p + 1)
                sp.dma_start(out_t[:, bass.ds(2 * p, 2), :], yb[par]).then_inc(y_out[par], 16)

            steps(sp, store, T // 2)
            for par in range(2):
                sp.wait_ge(y_out[par], 16 * T // 4)

        @block.gpsimd
        def _(pool):
            pool.memset(idf, 0.0).then_inc(ids, 1)
            pool.memset(idb, 0.0).then_inc(ids, 1)
            pool.memset(idh, 0.0).then_inc(ids, 1)
            pool.wait_ge(ids, 3)
            for m in (idf, idb, idh):
                pool.affine_select(out=m, in_=m, compare_op=ALU.not_equal, fill=1.0, base=0,
                                   pattern=[[-1, P]], channel_multiplier=1).then_inc(ids, 1)
            pool.memset(Vall, 0.0).then_inc(zeros, 1)
            pool.wait_ge(zeros, 1)
            for h2 in range(2):
                pool.memset(Vall[64 * h2:64 * h2 + 64, :, h2, HD:HD + 1], 1.0).then_inc(zeros, 1)

            pool.wait_ge(x2_ok, T)
            pool.iota(iota, pattern=[[1, P], [0, HALF]], base=0, channel_multiplier=0,
                      allow_small_or_imprecise_dtypes=True).then_inc(iota_ok, 1)
            pool.iota(iotaL, pattern=[[1, LO], [0, P]], base=0, channel_multiplier=0,
                      allow_small_or_imprecise_dtypes=True).then_inc(iota_ok, 1)
            pool.memset(planes, 0.0).then_inc(iota_ok, 1)
            pool.wait_ge(iota_ok, 3)

            def weight_rest(g):
                wait(pool, picks_sb, g + 1)
                pool.nop(nofuse=True)
                pool.tensor_tensor(wRest, wFull, w1[:, bass.ds(2 * g, 2), :], ALU.subtract).then_inc(rest_ok, 1)

            def sums(i, par):
                wait(pool, s8_ok, i + 1)
                pool.nop(nofuse=True)
                for at, ra, rb in BLOCKS:
                    na, nb = ra.stop - ra.start, rb.stop - rb.start
                    last = pool.tensor_tensor(cand[par][:, :, at:at + na * nb].rearrange("p h (a b) -> p h a b", a=na),
                                              rows(s8[par][:, 0, :, ra], nb),
                                              s8[par][:, 1, :, rb].unsqueeze(2).broadcast_to([P, FH, na, nb]), ALU.add)
                last.then_inc(cand_ok, 1)

            def differences(g):
                wait(pool, idx_ok, G4 * g + G4)
                pool.nop(nofuse=True)
                pool.tensor_scalar(i8f[:, 0], i8[:, 0], float(NK), 1.0, ALU.mult, ALU.mult).then_inc(poolc, 1)
                pool.tensor_copy(i8f[:, 1], i8[:, 1]).then_inc(poolc, 1)
                wait(pool, val_ok, g + 1)
                wait(pool, picks_ok, g)
                pool.tensor_tensor(wgt, val, rows(val[:, :, 0], K8), ALU.subtract).then_inc(diff_ok, 1)

            def codes(g):
                wait(pool, poolc, 2 * g + 2)
                wait(pool, planes_ok, g)
                for at, ra, rb in BLOCKS:
                    na, nb = ra.stop - ra.start, rb.stop - rb.start
                    last = pool.tensor_tensor(ccode[:, :, at:at + na * nb].rearrange("p t (a b) -> p t a b", a=na),
                                              rows(i8f[:, 0, :, ra], nb),
                                              i8f[:, 1, :, rb].unsqueeze(2).broadcast_to([P, G4 * FH, na, nb]), ALU.add)
                last.then_inc(ccode_ok, 1)

            def codes_of_picks(g, some):
                wait(pool, picks_hot, g + 1)
                wait(pool, ccode_ok, g + 1)
                pool.nop(nofuse=True)
                for c in some:
                    a, b = PAIRS[c]
                    k0 = (a + 1) * (b + 1) - 1
                    last = pool.tensor_tensor(planes[:, c, :, k0:K8], planes[:, c, :, k0:K8],
                                              rows(ccode[:, :, c], K8 - k0), ALU.mult)
                if c == NC - 1:
                    last.then_inc(planes_ok, 1)

            def weights(g):
                wait(pool, rsum_ok, g + 1)
                wait(pool, picks_T, g)
                pool.tensor_tensor(wnorm, wgt, rows(wsum, K8), ALU.mult).then_inc(picks_ok, 1)

            def during(G):
                g = G - 1
                differences(g)
                codes(g)
                sums(G4 * G, 0)
                if not (known(G) and G == 1):
                    weight_rest(G - 2)
                codes_of_picks(g, range(0, CUT1))
                sums(G4 * G + 1, 1)
                codes_of_picks(g, range(CUT1, CUT2))
                sums(G4 * G + 2, 0)
                codes_of_picks(g, range(CUT2, NC))
                weights(g)
                sums(G4 * G + 3, 1)

            CUT1, CUT2 = NC // 4, 3 * NC // 4
            for k in range(G4):
                sums(k, k % 2)
            during(1)
            with pool.Fori(2, T // G4) as G:
                during(G)
            differences(T // G4 - 1)
            codes(T // G4 - 1)
            weight_rest(T // G4 - 2)
            weights(T // G4 - 1)
            pool.wait_ge(picks_T, T // G4)
            pool.memset(oh, 0.0).then_inc(oh_zero, 1)
            weight_rest(T // G4 - 1)
            pool.wait_ge(split_ok, T // G4)
            pool.wait_ge(hl_ok, T // G4)
            pool.wait_ge(w_ok, T // G4)

            def lo_hots(p, buf, q):
                wait(pool, oh_ok, p + 1)
                wait(pool, p_ps, 4 * p + 2 * q - 6)
                pool.nop(nofuse=True)
                toks = slice(HALF * q, HALF * q + HALF)
                for part, w in enumerate((w1, w2)):
                    last = pool.tensor_tensor(Bm[buf][:, :, part, :, toks], oh[:, :, :, toks],
                                              w[:, bass.ds(p, 1), toks].unsqueeze(1).broadcast_to([P, 2, LO, HALF]), ALU.mult)
                last.then_inc(lo_hot, 1)

            def weigh(p, par, gi):
                wait(pool, pt_ok, 4 * p + gi + 1)
                wait(pool, gel_sb, 4 * p + 4)
                g = GG[par][:, :, :, Q32 * gi:Q32 * gi + Q32]
                pool.tensor_tensor(g, g, Pt[gi % 2], ALU.mult).then_inc(g_ok, 1)

            lo_hots(0, 0, 1)

            def step(p, j, par):
                more = not (isinstance(p, int) and p == T // 2 - 1)
                weigh(p, par, 0)
                weigh(p, par, 1)
                if more:
                    lo_hots(p + 1, 1 - par, 0)
                weigh(p, par, 2)
                weigh(p, par, 3)
                if more:
                    lo_hots(p + 1, 1 - par, 1)

            steps(pool, step, T // 2)

        @block.scalar
        def _(act):
            act.wait_ge(in_w, 16 * 13)
            act.activation(gates[:, 2:4], gates[:, 0:2], ACT.Tanh).then_inc(gates_ok, 1)
            act.wait_ge(std_in, 1)
            act.activation(lnt[:, 2, 0:XPIECE], lnt[:, 1, 0:XPIECE], ACT.Sqrt).then_inc(std_out, 1)

            def x_out(n):
                wait(act, x_T, n + 1)
                wait(act, q_ps, n)
                act.activation(xT, PS[:, 1, :], ACT.Copy).then_inc(x_T_sb, 1)

            def c_out(n):
                wait(act, c_T, n + 1)
                wait(act, v_ps, 2 * n)
                src = PS[:, 2, :].rearrange("p (t k) -> p t k", k=S)
                act.activation(cT.rearrange("p t b c k -> p (t b) c k"), src.unsqueeze(2).broadcast_to([P, 2 * G4, 2, S]),
                               ACT.Copy).then_inc(c_T_sb, 1)

            def q_high(n):
                wait(act, q_ps, n + 1)
                wait(act, q_wr, 16 * n)
                act.activation(QHL[:, 0], PS[:, 1, :], ACT.Copy).then_inc(q_hi, 1)

            def k_high(n):
                wait(act, k_ps, n + 1)
                wait(act, k_wr, 16 * n)
                act.activation(KHL[:, 0], PS[:, 2, :], ACT.Copy).then_inc(k_hi, 1)

            def v_out(n, gpar, pair):
                wait(act, v_ps, 2 * n + pair + 1)
                wait(act, av_ok, 4 * n - 4)
                for h2 in range(2):
                    r = slice(64 * h2, 64 * h2 + 64)
                    src = PS[r, 1, :].rearrange("p (m a d) -> p m a d", a=2, d=HD)[:, :, h2, :]
                    m0 = (gpar * G4 + 2 * pair) * 2 * HP
                    last = act.activation(Vall[r, m0:m0 + 4 * HP, h2, 0:HD], src, ACT.Copy)
                last.then_inc(v_sb, 1)

            def attn_out(i):
                wait(act, attn_T, i + 1)
                wait(act, wo_ok, i)
                act.activation(aT, PS[:, 0, 0:P], ACT.Copy).then_inc(attn_T_sb, 1)

            def ffn_out(k):
                src, dst = {0: (2, keyT.rearrange("p a b k -> p (a b k)")),
                            1: (1, kinT[:, 0:4].rearrange("p a b -> p (a b)")),
                            2: (2, kinT[:, 4:8].rearrange("p a b -> p (a b)")), 4: (1, W2)}[k]
                act.wait_ge(f_T, k + 1)
                act.activation(dst, PS[:, src, :], ACT.Copy).then_inc(f_T_sb, 1)

            x_out(0)
            c_out(0)
            q_high(0)
            k_high(0)
            act.wait_ge(zeros, 3)
            v_out(0, 0, 0)
            v_out(0, 0, 1)
            x_out(1)
            c_out(1)
            act.wait_ge(std_in, 2)
            act.activation(lnt[:, 2, XPIECE:], lnt[:, 1, XPIECE:], ACT.Sqrt).then_inc(std_out, 1)
            Ef = E.rearrange("p h k -> p (h k)")
            ETf = ET.rearrange("p h k -> p (h k)")

            def step(i, j, u):
                q, s, gpar = 2 * j + u // G4, u % G4, u // G4
                next1, next2 = not (known(i) and q + 1 >= NG), not (known(i) and q + 2 >= NG)
                if s == 3 and next2:
                    x_out(q + 2)
                for n in range(2):
                    wait(act, shifted, 2 * i + n + 1)
                    act.activation(Ef[:, 512 * n:512 * n + 512], Ef[:, 512 * n:512 * n + 512], ACT.Exp,
                                   scale=1.0 / SCORE).then_inc(probs, 1)
                    if s == 0 and next1:
                        (k_high if n else q_high)(q + 1)
                if not (known(i) and i < 2):
                    attn_out(i - 2)
                if s == 3 and next2:
                    c_out(q + 2)
                if s in (1, 2) and next1:
                    v_out(q + 1, 1 - gpar, s - 1)
                wait(act, av_ok, i)
                for n in range(2):
                    wait(act, e_T, 2 * i + n + 1)
                    act.activation(ETf[:, 512 * n:512 * n + 512], PS[:, 5 + n, :], ACT.Copy).then_inc(e_T_sb, 1)
                if known(i) and i >= T - 5 and i != T - 2:
                    ffn_out(i - (T - 5))

            group_steps(act, step)
            attn_out(T - 2)
            attn_out(T - 1)

            act.wait_ge(std_in, 3)
            act.activation(lnt[:, 2, :], lnt[:, 1, :], ACT.Sqrt).then_inc(std_out, 1)

            def normalise2(c, par):
                wait(act, z_T, c - 1)
                for k in range(2, 4):
                    i = 4 * c + k
                    last = act.activation(zb[par][:, k:k + 1, :], X[:, bass.ds(i, 1), :], ACT.Identity,
                                          bias=lnt[:, 0, bass.ds(i, 1)], scale=rstd[:, bass.ds(i, 1)])
                last.then_inc(z_act, 1)

            act.wait_ge(shift_ok, 1)
            normalise2(0, 0)

            def z_out(c, j, par):
                if not (isinstance(c, int) and c == T // 4 - 1):
                    normalise2(c + 1, 1 - par)
                wait(act, z_T, c + 1)
                act.activation(ZT[:, bass.ds(c * 512, 512)], PS[:, par, :], ACT.Copy).then_inc(z_sb, 1)

            steps(act, z_out, T // 4)
            act.wait_ge(std_in, 4)
            act.activation(bn[:, 7:8], bn[:, 4:5], ACT.Sqrt).then_inc(std_out, 1)
            act.wait_ge(bn_ok, 1)
            act.wait_ge(z_sb, T // 4)

            def picks_out(g):
                wait(act, picks_T, g + 1)
                wait(act, split_ok, g)
                wait(act, rest_ok, g)
                act.activation(codeT.rearrange("p a b -> p (a b)"), PS[:, 2, 0:256], ACT.Copy)
                weights = PS[:, 2, 256:512].rearrange("p (a b) -> p a b", a=2)
                act.activation(w1[:, bass.ds(2 * g, 2), :], weights, ACT.Copy, scale=W_SCALE)
                act.activation(wFull, weights, ACT.Copy, scale=W_SCALE).then_inc(picks_sb, 1)

            def lists_out(g):
                wait(act, split_ok, g + 1)
                act.activation(hi16[:, bass.ds(2 * g, 2), :], codeHL[:, 0], ACT.Copy)
                act.activation(lo16[:, bass.ds(2 * g, 2), :], codeHL[:, 1], ACT.Copy).then_inc(hl_ok, 1)
                wait(act, rest_ok, g + 1)
                act.activation(w2[:, bass.ds(2 * g, 2), :], wRest, ACT.Copy, scale=W2_SCALE).then_inc(w_ok, 1)

            def normed(i, par):
                wait(act, sim_ps, i - 1)
                act.activation(xs[par], ZT[:, bass.ds(i * P, P)], ACT.Identity, bias=bn[:, 6:7],
                               scale=bn[:, 5:6]).then_inc(xs_ok, 1)

            normed(0, 0)

            def exponentials(g):
                wait(act, diff_ok, g + 1)
                act.activation(wgt, wgt, ACT.Exp).then_inc(exp_ok, 1)

            def select(g, first=False, second=False, last=False):
                for k in range(G4):
                    i = G4 * g + k
                    if not (last and k == G4 - 1):
                        normed(i + 1, (k + 1) % 2)
                    wait(act, sim_ps, i + 1)
                    wait(act, idx_ok, i - 1)
                    act.activation(sim[k % 2].rearrange("p a h k -> p (a h k)"), PS[:, k % 2, :], ACT.Copy).then_inc(sim_sb, 1)
                    if k == 0 and not (first or second):
                        picks_out(g - 2)
                    if k == 1 and not first:
                        exponentials(g - 1)
                        if not second:
                            lists_out(g - 2)

            select(0, first=True)
            select(1, second=True)
            select(2)
            with act.Fori(3, T // G4 - 1) as g:
                select(g)
            select(T // G4 - 1, last=True)
            picks_out(T // G4 - 2)
            exponentials(T // G4 - 1)
            lists_out(T // G4 - 2)
            picks_out(T // G4 - 1)
            lists_out(T // G4 - 1)

            def second_part(p, gi):
                n = 4 * p + gi
                wait(act, p_ps, n + 1)
                wait(act, pt_ok, n - 1)
                act.activation(p2[gi % 2], placed(gi, 1),
                               ACT.Copy, scale=1.0 / W2_SCALE).then_inc(p2_sb, 1)

            def gelu(p, par, k):
                m = 4 * p + k
                wait(act, o_ps, m + 1)
                wait(act, f_ps, p - 1)
                act.activation(GG[par][:, 2 * k:2 * k + 2].rearrange("p l h t -> p (l h t)"), PS[:, 4 + k % 2, :],
                               ACT.Gelu).then_inc(gel_sb, 1)

            for k in range(4):
                gelu(0, 0, k)
            second_part(0, 0)
            second_part(0, 1)

            def step2(p, j, par):
                second_part(p, 2)
                second_part(p, 3)
                if not (isinstance(p, int) and p == T // 2 - 1):
                    for k in range(4):
                        gelu(p + 1, 1 - par, k)
                    second_part(p + 1, 0)
                    second_part(p + 1, 1)

            steps(act, step2, T // 2)

        @block.tensor
        def _(pe):
            pe.wait_ge(ids, 6)
            pe.wait_ge(in_w, 16 * 13)
            for n in range(4):
                last = pe.transpose(PS[:, 0, n * P:n * P + P], wnat[:, n, :], idf)
            last.then_inc(w_T, 1)
            pe.wait_ge(w_T_sb, 1)

            def inputs_T(n, par, loads):
                wait(pe, xn_ready, 4 * n + 4)
                wait(pe, q_sb, n)
                wait(pe, v_sb, 2 * n)
                for t in range(G4):
                    last = pe.transpose(PS[:, 1, t * P:t * P + P], xnb[:, t, :], idf)
                last.then_inc(x_T, 1)
                wait(pe, ctx_in[par], 16 * loads)
                wait(pe, k_sb, n)
                for t in range(G4):
                    last = pe.transpose(PS[:, 2, t * P:t * P + P], cb[par][:, t, :], idf)
                last.then_inc(c_T, 1)

            def project(n):
                wait(pe, x_T_sb, n + 1)
                pe.matmul(PS[:, 1, :], WqT.rearrange("p g r d -> p (g r d)"), xT, start=True, stop=True).then_inc(q_ps, 1)
                wait(pe, c_T_sb, n + 1)
                pe.matmul(PS[:, 2, :], WkT.rearrange("p g r d -> p (g r d)"), cT[:, :, :, 0, :], start=True,
                          stop=True).then_inc(k_ps, 1)

            def project_v(n, pair):
                wait(pe, c_T_sb, n + 1)
                wait(pe, q_sb, n + 1)
                wait(pe, v_sb, 2 * n + pair)
                for t in range(2):
                    for b in range(2):
                        last = pe.matmul(PS[:, 1, (2 * t + b) * P:(2 * t + b) * P + P],
                                         cT[:, 2 * pair + t, b].rearrange("p c k -> p (c k)"), WvT, start=True, stop=True)
                last.then_inc(v_ps, 1)

            def scores(i, j, u):
                q, s, gpar, par = 2 * j + u // G4, u % G4, u // G4, u % 2
                if s == 0:
                    wait(pe, qk_in, 128 * (q + 1))
                wait(pe, mask_ok, i + 1)
                wait(pe, rows_in[par], 32 * (4 * j + u // 2 + 1))
                wait(pe, shifted, 2 * i)
                for n in range(2):
                    o = PS[:, 3 + n, :]
                    pe.matmul(o, lrow[par], rrow[par][:, 512 * n:512 * n + 512], start=True, stop=False,
                              skip_group_check=True)
                    pe.matmul(o.rearrange("p (h k) -> p h k", k=S), idb, mb[par].unsqueeze(1).broadcast_to([P, 8, S]),
                              start=False, stop=False, skip_group_check=True)
                for k, r4 in enumerate((0, 2, 1, 3)):
                    if k >= 2:
                        pe.wait_ge(row_tile, 4 * i + k - 1)
                    n, r = r4 // 2, slice(32 * r4, 32 * r4 + 32)
                    for g in range(HG):
                        c = (4 * (r4 % 2) + g) * S
                        for b in range(2):
                            last = pe.matmul(PS[64 * b:64 * b + 64, 3 + n, c:c + S],
                                             Qp[gpar][r, g, P * s + 64 * b:P * s + 64 * b + 64],
                                             Kp[gpar][r, g, P * s + 64 * b:P * s + 64 * b + 64],
                                             start=False, stop=(k >= 2 and g == HG - 1), skip_group_check=True)
                    last.then_inc(row_tile, 1)

            def probs_T(i):
                for n in range(2):
                    wait(pe, probs, 2 * i + n + 1)
                    wait(pe, e_T_sb, 2 * i + n - 1)
                    for c in range(4):
                        p = 4 * n + c
                        last = pe.transpose(PS[:, 5 + n, c * P:c * P + P],
                                            E[:, 2 * p:2 * p + 2, :].rearrange("p h k -> p (h k)"), idf)
                    last.then_inc(e_T, 1)

            def values(i, u):
                wait(pe, e_T_sb, 2 * i + 2)
                wait(pe, attn_ok, i)
                for p in range(HP):
                    for b in range(2):
                        last = pe.matmul(PS[64 * b:64 * b + 64, 7, 18 * p:18 * p + 18], ET[:, p, 64 * b:64 * b + 64],
                                         Vt[:, u // G4, u % G4, b, p], start=True, stop=True)
                last.then_inc(av_ok, 1)

            def attn_turn(i):
                wait(pe, attn_ok, i + 1)
                wait(pe, x2_ok, i)
                pe.transpose(PS[:, 0, 0:P], attn.rearrange("p h d -> p (h d)"), idf).then_inc(attn_T, 1)

            def attn_wo(i):
                wait(pe, attn_T_sb, i + 1)
                pe.matmul(PS[:, 0, P:2 * P], aT, WoT, start=True, stop=True).then_inc(wo_ok, 1)

            def ffn_weights(k):
                if k == 0:
                    pe.wait_ge(k_sb, NG)
                    for n in range(4):
                        last = pe.transpose(PS[:, 2, n * P:n * P + P], keyn[:, n // 2, n % 2, :], idf)
                elif k < 3:
                    if k == 1:
                        pe.wait_ge(v_sb, 2 * NG)
                    else:
                        pe.wait_ge(f_T_sb, 1)
                    for n in range(4):
                        last = pe.transpose(PS[:, k, n * P:n * P + P], kinn[:, 4 * (k - 1) + n, :], idf)
                else:
                    pe.wait_ge(f_T_sb, 2)
                    a = k - 3
                    for h in range(FH):
                        c = (a * FH + h) * NK
                        last = pe.matmul(PS[:, 1, c:c + NK], wfn[:, a * FH + h, :],
                                         keyT[:, h // 4, a, (h % 4) * NK:(h % 4) * NK + NK], start=True, stop=True)
                last.then_inc(f_T, 1)

            inputs_T(0, 0, 1)
            project(0)
            project_v(0, 0)
            project_v(0, 1)
            inputs_T(1, 1, 1)
            pe.wait_ge(v_sb, 2)
            pe.wait_ge(c_T_sb, 2)
            pe.wait_ge(const_rows, 32)
            scores(0, 0, 0)

            def step(i, j, u):
                q, s, gpar = 2 * j + u // G4, u % G4, u // G4
                next1, next2 = not (known(i) and q + 1 >= NG), not (known(i) and q + 2 >= NG)
                if known(i) and i >= T - 5:
                    ffn_weights(i - (T - 5))
                if s == 3 and next2:
                    inputs_T(q + 2, gpar, j + 2)
                if s == 0 and next1:
                    project(q + 1)
                if s in (1, 2) and next1:
                    project_v(q + 1, s - 1)
                if not (known(i) and i == 0):
                    values(i - 1, (u - 1) % (2 * G4))
                if not (known(i) and i < 2):
                    attn_turn(i - 2)
                if u + 1 < 2 * G4:
                    scores(i + 1, j, u + 1)
                elif not (known(i) and i == T - 1):
                    scores(i + 1, j + 1, 0)
                if not (known(i) and i < 2):
                    attn_wo(i - 2)
                probs_T(i)

            group_steps(pe, step)
            values(T - 1, 2 * G4 - 1)
            attn_turn(T - 2)
            attn_wo(T - 2)
            attn_turn(T - 1)
            attn_wo(T - 1)

            pe.wait_ge(x2_ok, T)
            pe.wait_ge(f_T_sb, 4)

            def z_turn(c, j, par):
                wait(pe, z_ok, c + 1)
                wait(pe, z_act, c + 1)
                wait(pe, z_sb, c - 1)
                for k in range(4):
                    last = pe.transpose(PS[:, par, k * P:k * P + P], zb[par][:, k, :], idf)
                last.then_inc(z_T, 1)

            steps(pe, z_turn, T // 4)

            pe.wait_ge(z_sb, T // 4)
            pe.wait_ge(z_stat, T // 4)

            def picks_turn(g):
                wait(pe, picks_sb, g)
                if isinstance(g, int) and g == T // G4 - 1:
                    pe.wait_ge(planes_last, 1)
                else:
                    wait(pe, planes_ok, g + 1)
                for q in range(2):
                    cols = slice(16 * q, 16 * q + 16)
                    for c in range(NC):
                        pe.matmul(PS[:, 2, q * P:q * P + P], planes[:, c, cols, :].rearrange("p a b -> p (a b)"), idh,
                                  start=(c == 0), stop=(c == NC - 1))
                wait(pe, picks_ok, g + 1)
                for q in range(2):
                    cols = slice(16 * q, 16 * q + 16)
                    last = pe.transpose(PS[:, 2, 256 + q * P:256 + q * P + P],
                                        wnorm[:, cols, :].rearrange("p a b -> p (a b)"), idf)
                last.then_inc(picks_T, 1)

            def sims(g, early=False):
                for k in range(G4):
                    i = G4 * g + k
                    wait(pe, xs_ok, i + 1)
                    wait(pe, sim_sb, i - 1)
                    pe.matmul(PS[:, k % 2, :], xs[k % 2], W2, start=True, stop=True).then_inc(sim_ps, 1)
                    if k == 0 and not early:
                        picks_turn(g - 2)

            sims(0, early=True)
            sims(1, early=True)
            sims(2)
            with pe.Fori(3, T // G4) as g:
                sims(g)
            picks_turn(T // G4 - 2)
            picks_turn(T // G4 - 1)
            pe.wait_ge(picks_sb, T // G4)

            def expert_in(p, par, k):
                m = 4 * p + k
                wait(pe, gel_sb, m - 1)
                for n in range(2):
                    last = pe.matmul(PS[:, 4 + k % 2, n * 256:n * 256 + 256], kinT[:, 2 * k + n, :],
                                     ZT[:, bass.ds(p * 256, 256)], start=True, stop=True)
                last.then_inc(o_ps, 1)

            def place(p, par, gi):
                q = gi // 2
                n = 4 * p + gi
                wait(pe, a_ok, 2 * p + q + 1)
                if known(p) and p == 0 and q == 0:
                    pe.wait_ge(lo_first, 1)
                else:
                    wait(pe, lo_hot, 2 * p + q)
                wait(pe, pt_ok, n - 1)
                for t in range(Q32):
                    last = pe.matmul(PS[:, 2 * (gi % 2) + t // 16, 32 * (t % 16):32 * (t % 16) + 32],
                                     A[:, q, :, Q32 * (gi % 2) + t], Bm[par][:, :, :, :, Q32 * gi + t],
                                     start=True, stop=True)
                last.then_inc(p_ps, 1)

            def expert_out(p, par):
                wait(pe, g_ok, 4 * p + 4)
                wait(pe, y_ok, p)
                for half in range(2):
                    for l in range(LO):
                        last = pe.matmul(PS[:, 6, half * P:half * P + P], GG[par][:, l, half, :], kout[:, l, :],
                                         start=(l == 0), stop=(l == LO - 1))
                last.then_inc(f_ps, 1)

            for k in range(4):
                expert_in(0, 0, k)
            place(0, 0, 0)
            place(0, 0, 1)

            def step2(p, j, par):
                place(p, par, 2)
                place(p, par, 3)
                if not (isinstance(p, int) and p == 0):
                    expert_out(p - 1, 1 - par)
                if not (isinstance(p, int) and p == T // 2 - 1):
                    for k in range(4):
                        expert_in(p + 1, 1 - par, k)
                    place(p + 1, 1 - par, 0)
                    place(p + 1, 1 - par, 1)

            steps(pe, step2, T // 2)
            expert_out(T // 2 - 1, 1)

        @block.vector
        def _(dve):
            ch = Chain(dve, dve0)

            def layernorm_scale(done, tiles=slice(0, T)):
                me, m2e, mo, m2o = (stats[:, tiles, n] for n in (1, 2, 4, 5))
                mu, t0, t1 = mean[:, tiles], lnt[:, 0, tiles], lnt[:, 1, tiles]
                ch.add(dve.tensor_tensor(mu, me, mo, ALU.add))
                ch.add(dve.tensor_tensor(t0, me, mo, ALU.subtract))
                ch.add(dve.tensor_tensor(t1, m2e, m2o, ALU.add))
                ch.settle()
                ch.add(dve.tensor_scalar(mu, mu, 0.5, None, ALU.mult))
                ch.add(dve.tensor_tensor(t0, t0, t0, ALU.mult))
                ch.add(dve.tensor_scalar(t1, t1, 1.0 / D, EPS, ALU.mult, ALU.add))
                ch.settle()
                dve.scalar_tensor_tensor(t1, t0, 0.25, t1, ALU.mult, ALU.add).then_inc(std_in, 1)
                dve.wait_ge(std_out, done)
                ch.link(dve.reciprocal(rstd[:, tiles], lnt[:, 2, tiles]))

            dve.wait_ge(in_p, 64)
            ch.link(dve.tensor_copy(posF, posI))
            for h in range(H):
                ch.add(dve.tensor_scalar(kbias[:, h, :], posF[:, 1, :], SLOPES[h] * SCORE, None, ALU.mult))
            for par in range(2):
                ch.add(dve.tensor_copy(rrow[par][0:QROWS, :], srow_f))
            ch.add(dve.tensor_copy(brow_b, brow_f))
            ch.settle()
            kf = kbias.rearrange("p h k -> p (h k)")
            for n in range(3):
                ch.add(dve.tensor_copy(kparts[:, n, :], kf))
                ch.add(dve.tensor_copy(qparts[:, n, :], posF[:, 0, :]))
                ch.settle()
                if n < 2:
                    ch.add(dve.tensor_tensor(kf, kf, kparts[:, n, :], ALU.subtract))
                    ch.add(dve.tensor_tensor(posF[:, 0, :], posF[:, 0, :], qparts[:, n, :], ALU.subtract))
                    ch.settle()
            dve.sem_inc(parts_ok, 1)
            dve.wait_ge(zeros, 3)
            dve.wait_ge(w_T, 1)
            for n, (w, scale) in enumerate(((WqT, QK_SCALE / float(np.sqrt(HD))), (WkT, QK_SCALE))):
                dve.tensor_scalar(w, PS[:, 0, n * P:n * P + P].rearrange("p (r g d) -> p g r d", g=HG, r=4), scale, None,
                                  ALU.mult)
            dve.tensor_copy(WvT, PS[:, 0, 2 * P:3 * P])
            dve.tensor_copy(WoT, PS[:, 0, 3 * P:4 * P]).then_inc(w_T_sb, 1)
            dve.wait_ge(gates_ok, 1)
            ch.add(dve.tensor_scalar(gates[:, 3:4], gates[:, 3:4], 1.0 / W_SCALE, None, ALU.mult))
            def stats_of(tiles):
                for i in tiles:
                    if i % XPIECE == 0:
                        dve.wait_ge(in_x[i // XPIECE], 16)
                    dve.bn_stats(stats[:, i:i + 1, :], X[:, i:i + 1, :]).then_inc(stat_ok, 1)
                dve.wait_ge(stat_ok, tiles[-1] + 1)

            stats_of(range(XPIECE))
            layernorm_scale(1, slice(0, XPIECE))

            dve.wait_ge(in_m[0], 16)

            def normalise(i, n, t):
                if t == 0:
                    wait(dve, x_T, n)
                dve.tensor_scalar(xnb[:, t:t + 1, :], X[:, bass.ds(i, 1), :], mean[:, bass.ds(i, 1)], rstd[:, bass.ds(i, 1)],
                                  ALU.subtract, ALU.mult).then_inc(xn_ready, 1)

            def mask_term(i, par):
                wait(dve, row_tile, 4 * i - 4)
                dve.tensor_scalar(mb[par].unsqueeze(1), maskI[:, bass.ds(i, 1), :], 0.0, MASKED, ALU.is_equal,
                                  ALU.mult).then_inc(mask_ok, 1)

            def q_low(n):
                wait(dve, q_hi, n + 1)
                wait(dve, q_wr, 16 * n)
                dve.tensor_tensor(QHL[:, 1], PS[:, 1, :], QHL[:, 0], ALU.subtract).then_inc(q_sb, 1)

            def k_low(n):
                wait(dve, k_hi, n + 1)
                wait(dve, k_wr, 16 * n)
                dve.tensor_tensor(KHL[:, 1], PS[:, 2, :], KHL[:, 0], ALU.subtract).then_inc(k_sb, 1)

            def residual(i):
                wait(dve, wo_ok, i + 1)
                xi = X[:, bass.ds(i, 1), :]
                dve.scalar_tensor_tensor(xi, PS[:, 0, P:2 * P].unsqueeze(1), gates[:, 2:3], xi, ALU.mult,
                                         ALU.add).then_inc(x2_ok, 1)

            def stat(i):
                wait(dve, x2_ok, i + 1)
                dve.bn_stats(stats[:, bass.ds(i, 1), :], X[:, bass.ds(i, 1), :]).then_inc(stat_ok, 1)

            for t in range(G4):
                normalise(t, 0, t)
            mask_term(0, 0)
            for t in range(G4):
                normalise(G4 + t, 1, t)
            stats_of(range(XPIECE, 2 * XPIECE))
            q_low(0)
            k_low(0)
            stats_of(range(2 * XPIECE, 4 * XPIECE))
            stats_of(range(4 * XPIECE, T))
            layernorm_scale(2, slice(XPIECE, T))
            LINKS = 3
            link1 = Chain(dve, dve1)

            def step(i, j, u):
                q, s, par = 2 * j + u // G4, u % G4, u % 2
                ahead = not (known(i) and i + 2 * G4 >= T)
                if ahead and s == 3:
                    normalise(i + 2 * G4, q + 2, s)
                link1.at(0 if isinstance(i, int) and i == 0 else LINKS * i - 2)
                if isinstance(i, int) and i == 3:
                    dve.wait_ge(in_m[1], 16)
                wait(dve, row_tile, 4 * i + 4)
                sc = PS[:, 3:5, :].rearrange("p b (h k) -> p (b h) k", k=S)
                link1.add(dve.tensor_reduce(smax, sc, AX.X, ALU.max))
                if not (known(i) and i < 3):
                    residual(i - 3)
                if not (isinstance(i, int) and i == T - 1):
                    mask_term(i + 1, 1 - par)
                link1.settle()
                wait(dve, e_T, 2 * i)
                for n in range(2):
                    hs = slice(8 * n, 8 * n + 8)
                    dve.tensor_tensor(E[:, hs, :], sc[:, hs, :], rows(smax[:, hs], S), ALU.subtract).then_inc(shifted, 1)
                if not (known(i) and i < 3):
                    stat(i - 3)
                if ahead and s < 3:
                    normalise(i + 2 * G4, q + 2, s)
                if s == 0 and not (known(i) and q + 1 >= NG):
                    q_low(q + 1)
                    k_low(q + 1)
                if not (isinstance(i, int) and i == 0):
                    attended(i - 1)
                    assert link1.n == LINKS

            def attended(i):
                wait(dve, av_ok, i + 1)
                o = PS[:, 7, 0:144].rearrange("p (h e) -> p h e", e=HD + 1)
                link1.link(dve.tensor_scalar(den, o[:, :, HD], 1.0, None, ALU.add))
                link1.link(dve.reciprocal(den, den))
                wait(dve, attn_T, i)
                dve.tensor_tensor(attn, o[:, :, 0:HD], rows(den, HD), ALU.mult).then_inc(attn_ok, 1)

            group_steps(dve, step)
            link1.at(LINKS * T - 2)
            residual(T - 3)
            attended(T - 1)
            residual(T - 2)
            residual(T - 1)
            for i in range(T - 3, T):
                stat(i)

            dve.wait_ge(stat_ok, 2 * T)
            layernorm_scale(3)
            dve.scalar_tensor_tensor(lnt[:, 0, :], mean, -1.0, rstd, ALU.mult, ALU.mult).then_inc(shift_ok, 1)

            def normalise2(c, par):
                wait(dve, z_T, c - 1)
                for k in range(2):
                    i = 4 * c + k
                    last = dve.tensor_scalar(zb[par][:, k:k + 1, :], X[:, bass.ds(i, 1), :], mean[:, bass.ds(i, 1)],
                                             rstd[:, bass.ds(i, 1)], ALU.subtract, ALU.mult)
                last.then_inc(z_ok, 1)

            normalise2(0, 0)

            def statistics(c):
                wait(dve, z_sb, c + 1)
                dve.bn_stats(stats[:, bass.ds(c, 1), :], ZT[:, bass.ds(c * 512, 512)]).then_inc(z_stat, 1)

            def step1b(c, j, par):
                if not (isinstance(c, int) and c == T // 4 - 1):
                    normalise2(c + 1, 1 - par)
                if not (isinstance(c, int) and c == 0):
                    statistics(c - 1)

            steps(dve, step1b, T // 4)
            statistics(T // 4 - 1)
            dve.wait_ge(z_stat, T // 4)
            ch.link(dve.bn_aggr(bn[:, 2:4], stats[:, 0:T // 4, :].rearrange("p a b -> p (a b)")))
            dve.tensor_scalar(bn[:, 4:5], bn[:, 3:4], EPS, None, ALU.add).then_inc(std_in, 1)
            dve.wait_ge(std_out, 4)
            ch.link(dve.reciprocal(bn[:, 4:5], bn[:, 7:8]))
            ch.link(dve.tensor_tensor(bn[:, 5:6], bn[:, 4:5], bn[:, 0:1], ALU.mult))
            ch.link(dve.tensor_tensor(bn[:, 7:8], bn[:, 5:6], bn[:, 2:3], ALU.mult))
            dve.tensor_tensor(bn[:, 6:7], bn[:, 1:2], bn[:, 7:8], ALU.subtract).then_inc(bn_ok, 1)

            dve.wait_ge(iota_ok, 3)
            link2 = Chain(dve, dve2)

            def split(g):
                wait(dve, picks_sb, g + 1)
                wait(dve, hl_ok, g)
                dve.tensor_scalar(codeHL[:, 0], codeT, 3, None, ALU.logical_shift_right)
                dve.tensor_scalar(codeHL[:, 1], codeT, LO - 1, None, ALU.bitwise_and).then_inc(split_ok, 1)

            def hi_hots(p, q):
                wait(dve, p_ps, 4 * p + 2 * q - 2)
                src = hi16[:, bass.ds(p, 1), HALF * q:HALF * q + HALF]
                for n in range(2):
                    v = slice(64 * n, 64 * n + 64)
                    last = dve.tensor_tensor(A[:, q, v, :], src.broadcast_to([P, 64, HALF]), iota[:, v, :], ALU.is_equal)
                last.then_inc(a_ok, 1)

            def pick(k):
                for h in range(FH):
                    last = dve.max_index(pk[:, k * FH + h, :], val[:, k * FH + h, :], cand[k % 2][:, h])
                link2.add(last)

            def decode(g, last_group=False):
                if last_group:
                    dve.wait_ge(ccode_ok, T // G4)
                wait(dve, picks_T, g)
                link2.settle()
                for c, (a, b) in enumerate(PAIRS):
                    k0 = (a + 1) * (b + 1) - 1
                    if last_group:
                        last = dve.scalar_tensor_tensor(planes[:, c, :, k0:K8], pk[:, :, k0:K8], float(c),
                                                        rows(ccode[:, :, c], K8 - k0), ALU.is_equal, ALU.mult)
                    else:
                        last = dve.tensor_scalar(planes[:, c, :, k0:K8], pk[:, :, k0:K8], float(c), None, ALU.is_equal)
                last.then_inc(planes_last if last_group else picks_hot, 1)
                wait(dve, exp_ok, g + 1)
                wait(dve, picks_ok, g)
                link2.add(dve.tensor_reduce(wsum, wgt, AX.X, ALU.add))

            def select(g, first=False, second=False):
                for k in range(G4):
                    i = G4 * g + k
                    par = k % 2
                    wait(dve, sim_sb, i + 1)
                    dve.nop(nofuse=True)
                    for a in range(2):
                        for h in range(FH):
                            last = dve.max(s8[par][:, a, h, :], sim[par][:, a, h, :])
                    last.then_inc(s8_ok, 1)
                    if not (first and k == 0):
                        link2.settle()
                        dve.nop(nofuse=True)
                        pick((k - 1) % G4)
                    wait(dve, s8_ok, i + 1)
                    dve.nop(nofuse=True)
                    if k == 0:
                        wait(dve, poolc, 2 * g)
                        dve.nop(nofuse=True)
                    for a in range(2):
                        for h in range(FH):
                            last = dve.max_index(i8[:, a, k * FH + h, :], s8[par][:, a, h, :], sim[par][:, a, h, :])
                    last.then_inc(idx_ok, 1)
                    if k == 0 and not first:
                        decode(g - 1)
                    wait(dve, cand_ok, i + 1)
                    if k == 0:
                        wait(dve, diff_ok, g)
                    dve.nop(nofuse=True)
                    for h in range(FH):
                        last = dve.max(val[:, k * FH + h, :], cand[par][:, h])
                    link2.add(last)
                    if k == G4 - 1:
                        link2.settle()
                        dve.sem_inc(val_ok, 1)
                    if k == 0 and not first:
                        link2.settle(but=1)
                        dve.reciprocal(wsum, wsum).then_inc(rsum_ok, 1)
                    if k == 0 and not (first or second):
                        split(g - 2)

            EACH = 2 * G4 + 1
            link2.at(0)
            select(0, first=True)
            assert link2.n == EACH - 2, link2.n
            link2.at(EACH - 2)
            select(1, second=True)
            link2.at(2 * EACH - 2)
            select(2)
            link2.at(3 * EACH - 2)
            select(3)
            with dve.Fori(2, T // G4 // 2) as pair:
                for g in (2 * pair, 2 * pair + 1):
                    link2.at(g * EACH - 2)
                    select(g)
                    assert link2.n == EACH, link2.n
            link2.at(EACH * (T // G4) - 2)
            link2.settle()
            pick(G4 - 1)
            decode(T // G4 - 1, last_group=True)
            link2.settle()
            dve.reciprocal(wsum, wsum).then_inc(rsum_ok, 1)
            split(T // G4 - 2)
            hi_hots(0, 0)
            split(T // G4 - 1)
            dve.wait_ge(hl_ok, T // G4)
            dve.wait_ge(oh_zero, 1)

            def joined(p, gi):
                n = 4 * p + gi
                wait(dve, p2_sb, n + 1)
                wait(dve, g_ok, n - 1)
                dve.tensor_tensor(Pt[gi % 2], placed(gi, 0), p2[gi % 2], ALU.add).then_inc(pt_ok, 1)

            def finish(p, j, par):
                wait(dve, f_ps, p + 1)
                wait(dve, y_out[par], 16 * j)
                dve.scalar_tensor_tensor(yb[par], PS[:, 6, 0:256].rearrange("p (a d) -> p a d", a=2), gates[:, 3:4],
                                         X[:, bass.ds(2 * p, 2), :], ALU.mult, ALU.add).then_inc(y_ok, 1)

            def lo_ones(p):
                wait(dve, lo_hot, 2 * p - 1)
                for half in range(2):
                    r = slice(64 * half, 64 * half + 64)
                    last = dve.tensor_tensor(oh[r, half], lo16[r, bass.ds(p, 1), :].broadcast_to([64, LO, P]), iotaL[r],
                                             ALU.is_equal)
                last.then_inc(oh_ok, 1)

            lo_ones(0)
            dve.wait_ge(w_ok, T // G4)
            dve.wait_ge(oh_ok, 1)
            for part, w in enumerate((w1, w2)):
                last = dve.tensor_tensor(Bm[0][:, :, part, :, 0:HALF], oh[:, :, :, 0:HALF],
                                         w[:, 0:1, 0:HALF].unsqueeze(1).broadcast_to([P, 2, LO, HALF]), ALU.mult)
            last.then_inc(lo_first, 1)
            hi_hots(0, 1)

            def step2(p, j, par):
                more = not (isinstance(p, int) and p == T // 2 - 1)
                joined(p, 0)
                joined(p, 1)
                if more:
                    lo_ones(p + 1)
                    hi_hots(p + 1, 0)
                joined(p, 2)
                joined(p, 3)
                if not (isinstance(p, int) and p == 0):
                    finish(p - 1, j if par else j - 1, 1 - par)
                if more:
                    hi_hots(p + 1, 1)

            steps(dve, step2, T // 2, lead=4)
            finish(T // 2 - 1, T // 4 - 1, 1)


_INS = ["x", "ctx_1024", "itok_BxS_8_8191", "itok_BxS2_1_8191", "mask_BxSxS2_if1", "g_xattn", "g_ffn", "L0_xattn_W_q",
        "L0_xattn_W_k", "L0_xattn_W_v", "L0_xattn_W_o", "L0_ffn_gamma", "L0_ffn_beta", "L0_ffn_w_q", "L0_ffn_keys",
        "L0_ffn_key_in", "L0_ffn_key_out"]


def kernel(**inputs):
    import concourse.bacc as bacc
    from concourse.bass_utils import run_bass_kernel_spmd

    nc = bacc.Bacc("TRN2", target_bir_lowering=False, num_devices=1)
    arrays, args = {}, []
    given = [(n, inputs[n]) for n in _INS] + list(zip(("slope_rows", "of_batch"), shape_constants()))
    for name, a in given:
        a = np.ascontiguousarray(a)
        arrays[f"in_{name}"] = a
        args.append(nc.dram_tensor(f"in_{name}", a.shape, mybir.dt.from_np(a.dtype), kind="ExternalInput").ap())
    args.append(nc.dram_tensor("out_0", (B, S, D), F32, kind="ExternalOutput").ap())
    gated_block(nc, *args)
    r = run_bass_kernel_spmd(nc, [arrays], core_ids=[0])
    return r.results[0]["out_0"]
```
